# Optimizing a Trainium2 kernel written in Bass

```python
import numpy as np
import jax
import jax.numpy as jnp

def _softmax(x, axis=-1):
    return jax.nn.softmax(x, axis=axis)

def _gelu(x):
    return jax.nn.gelu(x, approximate=True)

def _silu(x):
    return jax.nn.silu(x)

def _sigmoid(x):
    return jax.nn.sigmoid(x)

def _layernorm(x, axis=-1, eps=1e-05):
    m = jnp.mean(x, axis=axis, keepdims=True)
    v = jnp.var(x, axis=axis, keepdims=True)
    return (x - m) / jnp.sqrt(v + eps)

def _scatter_add(tgt, idx, src, axis=0):
    return tgt.at[idx].add(src)

def _segment_sum(src, seg, n):
    return jax.ops.segment_sum(src, seg, n)
kernel_name = 'mk_flamingo_gated_d1_seqx_r8_929586'

def setup_inputs(seed: int=0):
    np.random.seed(seed)
    _w = jnp.asarray

    def _rec_inputs():
        import jax
        import jax.numpy as jnp
        _rk = jax.random.key(seed)
        x = 7.22e-05 + 1 * jax.random.normal(jax.random.fold_in(_rk, 1), (8, 128, 256), jnp.float32)
        _lenS = 128 - jax.random.randint(jax.random.fold_in(_rk, 7), (8,), 0, max(1, 128 // 4) + 1, jnp.int32)
        _lenS2 = 128 - jax.random.randint(jax.random.fold_in(_rk, 8), (8,), 0, max(1, 128 // 4) + 1, jnp.int32)
        _ctx_1024P = jax.random.normal(jax.random.fold_in(_rk, 11), (8, 16, 128), jnp.float32)
        _ctx_1024c = jax.random.dirichlet(jax.random.fold_in(_rk, 511), 0.3 * jnp.ones((16,), jnp.float32), (8, 128))
        _ctx_1024t = jnp.einsum('bsk,bkd->bsd', _ctx_1024c, _ctx_1024P)
        _ctx_1024t = _ctx_1024t * jax.lax.rsqrt(jnp.mean(jnp.square(_ctx_1024t)) + 1e-12) * 0.953939
        ctx_1024 = -0.000673644 + 1.00013 * (_ctx_1024t + 0.3 * jax.random.normal(jax.random.fold_in(_rk, 611), (8, 128, 128), jnp.float32))
        _g = jax.random.normal(jax.random.fold_in(_rk, 9001), (2, 1), jnp.float32)
        _g = jnp.sign(_g) * jnp.maximum(jnp.abs(_g), 1.0) + (_g == 0) * 1.0
        g_xattn = _g[0]
        g_ffn = _g[1]
        return (x, ctx_1024, g_xattn, g_ffn)
    x, ctx_1024, g_xattn, g_ffn = _rec_inputs()

    def _L0_xattn_setup():
        import jax, jax.numpy as jnp
        import numpy as np
        B, S1, S2, DCA = (2, 256, 128, 16)
        QDIM, KDIM, H = (256, 128, 16)
        HD = QDIM // H
        SCALE = HD ** (-0.5)
        EPS = 1e-06
        DCA_WEIGHT = 1.0

        def _ln(t, w, b):
            m = jnp.mean(t, axis=-1, keepdims=True)
            v = jnp.var(t, axis=-1, keepdims=True)
            return (t - m) * jax.lax.rsqrt(v + EPS) * w + b

        def _attn(q, k, v):
            s = jnp.einsum('bhqd,bhkd->bhqk', q, k) * SCALE
            p = jax.nn.softmax(s, axis=-1)
            return jnp.einsum('bhqk,bhkd->bhqd', p, v)
        key = jax.random.key(seed)
        ks = jax.random.split(key, 8)
        w = lambda k, shape: jax.random.normal(k, shape, jnp.float32) * 0.02
        return {'x': jax.random.normal(ks[0], (B, S1, QDIM), jnp.float32), 'y': jax.random.normal(ks[1], (B, S2 + DCA, KDIM), jnp.float32), 'Wq': w(ks[2], (QDIM, QDIM)), 'bq': jnp.zeros((QDIM,), jnp.float32), 'Wk': w(ks[3], (KDIM, QDIM)), 'bk': jnp.zeros((QDIM,), jnp.float32), 'Wv': w(ks[4], (KDIM, QDIM)), 'bv': jnp.zeros((QDIM,), jnp.float32), 'Wkv_dca': w(ks[5], (KDIM, 2 * QDIM)), 'bkv_dca': jnp.zeros((2 * QDIM,), jnp.float32), 'qn_w': jnp.ones((HD,), jnp.float32), 'qn_b': jnp.zeros((HD,), jnp.float32), 'kn_w': jnp.ones((HD,), jnp.float32), 'kn_b': jnp.zeros((HD,), jnp.float32), 'kn_dca_w': jnp.ones((HD,), jnp.float32), 'kn_dca_b': jnp.zeros((HD,), jnp.float32), 'Wo': w(ks[6], (QDIM, QDIM)), 'bo': jnp.zeros((QDIM,), jnp.float32)}
    _L0_xattn_all = _L0_xattn_setup()
    _L0_xattn_in = {k: v for k, v in _L0_xattn_all.items() if k in ('Wq', 'bq', 'Wk', 'bk', 'Wv', 'bv', 'Wkv_dca', 'bkv_dca', 'qn_w', 'qn_b', 'kn_w', 'kn_b', 'kn_dca_w', 'kn_dca_b', 'Wo', 'bo')}
    del _L0_xattn_all

    def _L0_ffn_setup():
        import jax, jax.numpy as jnp
        import numpy as np
        from jax import lax
        D_MODEL = 256
        D_CROSS = 1024
        D_RETR = 128
        D_PRIV = 128
        N_EXPERTS = 2048
        N_HEADS = 8
        K_PER_HEAD = 8
        NUM_KEYS = int(np.sqrt(N_EXPERTS))
        BATCH, SEQ = (2, 256)
        key = jax.random.key(seed)
        ks = jax.random.split(key, 10)
        s = 0.02
        return {'hidden_states': jax.random.normal(ks[0], (BATCH, SEQ, D_MODEL), jnp.float32), 'W_up': jax.random.normal(ks[1], (D_CROSS, D_MODEL), jnp.float32) * s, 'b_up': jnp.zeros((D_CROSS,), jnp.float32), 'W_down': jax.random.normal(ks[2], (D_PRIV, D_CROSS), jnp.float32) * s, 'b_down': jnp.zeros((D_PRIV,), jnp.float32), 'W_q': jax.random.normal(ks[3], (D_RETR * N_HEADS, D_PRIV), jnp.float32) * s, 'keys': jax.random.normal(ks[4], (N_HEADS, NUM_KEYS, 2, D_RETR // 2), jnp.float32) * s, 'down_embed': jax.random.normal(ks[5], (N_EXPERTS, D_PRIV), jnp.float32) * s, 'up_embed': jax.random.normal(ks[6], (N_EXPERTS, D_MODEL), jnp.float32) * s}
    _L0_ffn_all = _L0_ffn_setup()
    _L0_ffn_in = {k: v for k, v in _L0_ffn_all.items() if k in ('W_up', 'b_up', 'W_down', 'b_down', 'W_q', 'keys', 'down_embed', 'up_embed')}
    del _L0_ffn_all
    return {'x': x, 'ctx_1024': ctx_1024, 'g_xattn': g_xattn, 'g_ffn': g_ffn, 'L0_xattn_Wq': _L0_xattn_in['Wq'], 'L0_xattn_bq': _L0_xattn_in['bq'], 'L0_xattn_Wk': _L0_xattn_in['Wk'], 'L0_xattn_bk': _L0_xattn_in['bk'], 'L0_xattn_Wv': _L0_xattn_in['Wv'], 'L0_xattn_bv': _L0_xattn_in['bv'], 'L0_xattn_Wkv_dca': _L0_xattn_in['Wkv_dca'], 'L0_xattn_bkv_dca': _L0_xattn_in['bkv_dca'], 'L0_xattn_qn_w': _L0_xattn_in['qn_w'], 'L0_xattn_qn_b': _L0_xattn_in['qn_b'], 'L0_xattn_kn_w': _L0_xattn_in['kn_w'], 'L0_xattn_kn_b': _L0_xattn_in['kn_b'], 'L0_xattn_kn_dca_w': _L0_xattn_in['kn_dca_w'], 'L0_xattn_kn_dca_b': _L0_xattn_in['kn_dca_b'], 'L0_xattn_Wo': _L0_xattn_in['Wo'], 'L0_xattn_bo': _L0_xattn_in['bo'], 'L0_ffn_W_up': _L0_ffn_in['W_up'], 'L0_ffn_b_up': _L0_ffn_in['b_up'], 'L0_ffn_W_down': _L0_ffn_in['W_down'], 'L0_ffn_b_down': _L0_ffn_in['b_down'], 'L0_ffn_W_q': _L0_ffn_in['W_q'], 'L0_ffn_keys': _L0_ffn_in['keys'], 'L0_ffn_down_embed': _L0_ffn_in['down_embed'], 'L0_ffn_up_embed': _L0_ffn_in['up_embed']}

def reference(x, ctx_1024, g_xattn, g_ffn, L0_xattn_Wq, L0_xattn_bq, L0_xattn_Wk, L0_xattn_bk, L0_xattn_Wv, L0_xattn_bv, L0_xattn_Wkv_dca, L0_xattn_bkv_dca, L0_xattn_qn_w, L0_xattn_qn_b, L0_xattn_kn_w, L0_xattn_kn_b, L0_xattn_kn_dca_w, L0_xattn_kn_dca_b, L0_xattn_Wo, L0_xattn_bo, L0_ffn_W_up, L0_ffn_b_up, L0_ffn_W_down, L0_ffn_b_down, L0_ffn_W_q, L0_ffn_keys, L0_ffn_down_embed, L0_ffn_up_embed):
    import jax
    import jax.numpy as jnp

    def _L0_xattn_ref(x, y, Wq, bq, Wk, bk, Wv, bv, Wkv_dca, bkv_dca, qn_w, qn_b, kn_w, kn_b, kn_dca_w, kn_dca_b, Wo, bo):
        import jax, jax.numpy as jnp
        import numpy as np
        B, S1, S2, DCA = (2, 256, 128, 16)
        QDIM, KDIM, H = (256, 128, 16)
        HD = QDIM // H
        SCALE = HD ** (-0.5)
        EPS = 1e-06
        DCA_WEIGHT = 1.0

        def _ln(t, w, b):
            m = jnp.mean(t, axis=-1, keepdims=True)
            v = jnp.var(t, axis=-1, keepdims=True)
            return (t - m) * jax.lax.rsqrt(v + EPS) * w + b

        def _attn(q, k, v):
            s = jnp.einsum('bhqd,bhkd->bhqk', q, k) * SCALE
            p = jax.nn.softmax(s, axis=-1)
            return jnp.einsum('bhqk,bhkd->bhqd', p, v)
        b, s1, _ = x.shape
        y_dca = y[:, -DCA:, :]
        y_main = y[:, :-DCA, :]
        kv_dca = (y_dca @ Wkv_dca + bkv_dca).reshape(b, DCA, 2, H, HD)
        k_dca = _ln(kv_dca[:, :, 0], kn_dca_w, kn_dca_b)
        v_dca = kv_dca[:, :, 1]
        s2 = y_main.shape[1]
        q = _ln((x @ Wq + bq).reshape(b, s1, H, HD), qn_w, qn_b)
        kv = jnp.concatenate([y_main @ Wk + bk, y_main @ Wv + bv], axis=-1)
        kv = kv.reshape(b, s2, H, 2 * HD)
        k = _ln(kv[..., :HD], kn_w, kn_b)
        v = kv[..., HD:]
        qT = q.transpose(0, 2, 1, 3)
        ctx = _attn(qT, k.transpose(0, 2, 1, 3), v.transpose(0, 2, 1, 3))
        ctx = ctx.transpose(0, 2, 1, 3).reshape(b, s1, QDIM)
        ctx_dca = _attn(qT, k_dca.transpose(0, 2, 1, 3), v_dca.transpose(0, 2, 1, 3))
        ctx_dca = ctx_dca.transpose(0, 2, 1, 3).reshape(b, s1, QDIM)
        ctx = ctx + DCA_WEIGHT * ctx_dca
        return ctx @ Wo + bo

    def _L0_ffn_ref(hidden_states, W_up, b_up, W_down, b_down, W_q, keys, down_embed, up_embed):
        import jax, jax.numpy as jnp
        import numpy as np
        from jax import lax
        D_MODEL = 256
        D_CROSS = 1024
        D_RETR = 128
        D_PRIV = 128
        N_EXPERTS = 2048
        N_HEADS = 8
        K_PER_HEAD = 8
        NUM_KEYS = int(np.sqrt(N_EXPERTS))
        BATCH, SEQ = (2, 256)
        b, t, _ = hidden_states.shape
        act = jax.nn.silu
        h = act(jnp.einsum('btd,cd->btc', hidden_states, W_up) + b_up)
        h = jnp.einsum('btc,pc->btp', h, W_down) + b_down
        q = jnp.einsum('btp,rp->btr', h, W_q)
        q = q.reshape(b, t, 2, N_HEADS, D_RETR // 2).transpose(2, 0, 1, 3, 4)
        sim = jnp.einsum('pbthn,hkpn->pbthk', q, keys)
        scores, idx = lax.top_k(sim, K_PER_HEAD)
        sx, sy = (scores[0], scores[1])
        ix, iy = (idx[0], idx[1])
        all_scores = (sx[..., :, None] + sy[..., None, :]).reshape(b, t, N_HEADS, K_PER_HEAD * K_PER_HEAD)
        all_indices = (ix[..., :, None] * NUM_KEYS + iy[..., None, :]).reshape(b, t, N_HEADS, K_PER_HEAD * K_PER_HEAD)
        sc, pk = lax.top_k(all_scores, K_PER_HEAD)
        indices = jnp.take_along_axis(all_indices, pk, axis=-1)
        de = down_embed[indices]
        ue = up_embed[indices]
        z = jnp.einsum('btd,bthkd->bthk', h, de)
        z = act(z * jax.nn.softmax(sc, axis=-1))
        out = jnp.einsum('bthk,bthkd->btd', z, ue)
        return out
    x = x + jnp.tanh(g_xattn[0]) * _L0_xattn_ref(_layernorm(x, axis=-1), ctx_1024, L0_xattn_Wq, L0_xattn_bq, L0_xattn_Wk, L0_xattn_bk, L0_xattn_Wv, L0_xattn_bv, L0_xattn_Wkv_dca, L0_xattn_bkv_dca, L0_xattn_qn_w, L0_xattn_qn_b, L0_xattn_kn_w, L0_xattn_kn_b, L0_xattn_kn_dca_w, L0_xattn_kn_dca_b, L0_xattn_Wo, L0_xattn_bo)
    x = x + jnp.tanh(g_ffn[0]) * _L0_ffn_ref(_layernorm(x, axis=-1), L0_ffn_W_up, L0_ffn_b_up, L0_ffn_W_down, L0_ffn_b_down, L0_ffn_W_q, L0_ffn_keys, L0_ffn_down_embed, L0_ffn_up_embed)
    return x

_drawn_inputs = setup_inputs


def setup_inputs(seed=0):
    import zlib

    import numpy as np

    out = dict(_drawn_inputs(seed))
    spreads = {'L0_xattn_bq': (0.0, 0.8),
     'L0_xattn_bk': (0.0, 0.527),
     'L0_xattn_bv': (0.0, 0.433),
     'L0_xattn_bkv_dca': (0.0, 0.32),
     'L0_xattn_qn_w': (1.0, 0.6),
     'L0_xattn_qn_b': (0.0, 0.8),
     'L0_xattn_kn_w': (1.0, 0.6),
     'L0_xattn_kn_b': (0.0, 0.8),
     'L0_xattn_kn_dca_w': (1.0, 0.6),
     'L0_xattn_kn_dca_b': (0.0, 0.8),
     'L0_xattn_bo': (0.0, 0.1),
     'L0_ffn_b_up': (0.0, 0.8),
     'L0_ffn_b_down': (0.0, 0.8)}
    factors = {'L0_xattn_Wq': 3.234,
     'L0_xattn_Wk': 2.694,
     'L0_xattn_Wv': 2.822,
     'L0_ffn_W_up': 8.0,
     'L0_ffn_W_down': 8.0,
     'L0_ffn_W_q': 8.0,
     'L0_ffn_keys': 8.0,
     'L0_ffn_down_embed': 8.0,
     'L0_ffn_up_embed': 8.0}
    for name, (base, spread) in spreads.items():
        noise = np.random.default_rng([zlib.crc32(name.encode()), seed]).standard_normal(out[name].shape)
        drawn = base * np.exp(spread * noise) if base else spread * noise
        out[name] = jnp.asarray(drawn.astype(out[name].dtype))
    for name, factor in factors.items():
        out[name] = (out[name] * factor).astype(out[name].dtype)
    return out
```

```python
from contextlib import ExitStack

import concourse.bass as bass
from concourse import mybir


def gated_xattn_peer_kernel(
    nc: bass.Bass,
    x: bass.AP,
    y_t: bass.AP,
    gates: bass.AP,
    w_q: bass.AP,
    b_q: bass.AP,
    w_kv: bass.AP,
    b_kv: bass.AP,
    ln_wb: bass.AP,
    w_o: bass.AP,
    b_o: bass.AP,
    w_up_t: bass.AP,
    b_up: bass.AP,
    w_down_t: bass.AP,
    b_down: bass.AP,
    w_ret: bass.AP,
    keys_t: bass.AP,
    down_t: bass.AP,
    up: bass.AP,
    lo_scratch: bass.AP,
    out: bass.AP,
):
    f32 = mybir.dt.float32
    bf16 = mybir.dt.bfloat16
    u32 = mybir.dt.uint32
    ALU = mybir.AluOpType
    ACT = mybir.ActivationFunctionType
    X = mybir.AxisListType.X

    P = 128
    B, S, D = x.shape
    DY, KEYS = y_t.shape[1:]
    DCA = 16
    MAIN = KEYS - DCA
    H, HD = 16, D // 16
    G = D // P
    HG = H // G
    DC = w_up_t.shape[1]
    NC = DC // P
    NK = keys_t.shape[2]
    NH, K = 8, 8
    HK = NH * K
    NE = 2048
    EC = NE // P
    PAIRS = P // 2
    QP = 16
    GROUP = 512
    EPS_X, EPS_QK = 1e-5, 1e-6
    SCALE = HD ** -0.5

    ctx = ExitStack()
    with ctx:
        def sb(name, shape, dt=f32):
            return ctx.enter_context(nc.sbuf_tensor(name, shape, dt))

        def ps(name, shape, dt=f32):
            return ctx.enter_context(nc.psum_tensor(name, shape, dt))

        def sem(name):
            return ctx.enter_context(nc.semaphore(name))

        ident = sb("ident", [P, P])
        head_mask = sb("head_mask", [P, HG])
        iota_p = sb("iota_p", [P, 1])
        iota8 = sb("iota8", [P, K])
        iota_hi = sb("iota_hi", [P, 2 * EC, PAIRS], bf16)
        iota_lo = sb("iota_lo", [P, P, PAIRS], bf16)
        minus_half = sb("minus_half", [P, 2 * H])
        wq_sb = sb("wq_sb", [P, G, D])
        wkv_sb = sb("wkv_sb", [P, 2, 2 * D])
        bqkv = sb("bqkv", [P, 3 * D])
        wb = sb("wb", [P, 6])
        wo_sb = sb("wo_sb", [P, G, D])
        bo_t = sb("bo_t", [P, D])
        gate_in = sb("gate_in", [P, 2])
        gate = sb("gate", [P, 2])
        bup_sb = sb("bup_sb", [P, NC])
        bdown_sb = sb("bdown_sb", [P, 1])
        keys_sb = sb("keys_sb", [P, 8, NK])
        simw = sb("simw", [P, 2 * NH * NK])
        down_sb = sb("down_sb", [P, EC, P])
        up_sb = sb("up_sb", [P, EC, D])
        means = sb("means", [P, 6, H])

        area = sb("area", [P, 6 * H * P])

        def attention_area(i, *shape):
            v = area[:, i * H * P:(i + 1) * H * P]
            return v.rearrange("p (g h c) -> p g h c", g=G, c=P) if shape == (G, HG, P) else v.rearrange("p (h c) -> p h c", h=shape[0])

        def mask_area(i, a, b):
            return area[:, i * PAIRS * P // 2:(i + 1) * PAIRS * P // 2].bitcast(bf16).rearrange("p (a b) -> p a b", a=a)

        ffn = sb("ffn", [P, 8192])
        heads_v = sb("heads_v", [P, G * HG * (P + HD)])

        x_sb = attention_area(0, B, D)
        x1 = sb("x1", [P, B, D])
        xstat = sb("xstat", [P, B, 6])
        xmv = sb("xmv", [P, B, 2])
        xvar = sb("xvar", [P, B])
        xrstd = sb("xrstd", [P, B])
        xn = sb("xn", [P, D])
        xn_t = sb("xn_t", [P, G, P])
        y_main = sb("y_main", [P, P])
        y_dca = sb("y_dca", [P, P])
        qk = sb("qk", [P, 2 * H, HD])
        v_sb = sb("v_sb", [P, D])
        qk_sq = sb("qk_sq", [P, 2 * H, HD])
        qk_ss = sb("qk_ss", [P, 2 * H])
        qk_var = sb("qk_var", [P, 2 * H])
        qk_rstd = sb("qk_rstd", [P, 2 * H])
        qkn = sb("qkn", [P, 2 * H, HD])
        q_t = sb("q_t", [P, G, P])
        k_t = sb("k_t", [P, G, P])
        k_diag = attention_area(1, G, HG, P)
        v_diag = heads_v[:, :].rearrange("p (g c) -> p g c", g=G)
        smax = sb("smax", [P, 2, H])
        shifted = attention_area(2, H, P)
        prob = attention_area(3, H, P)
        ssum = sb("ssum", [P, 2, H])
        rsum = sb("rsum", [P, 2, H])
        pnorm = attention_area(4, H, P)
        prob_t = attention_area(5, H, P)
        ctx_t = sb("ctx_t", [P, G, P])
        stat1 = sb("stat1", [P, 6])
        mv1 = sb("mv1", [P, 2])
        var1 = sb("var1", [P, 1])
        rstd1 = sb("rstd1", [P, 1])
        xn1 = sb("xn1", [P, D])
        xn1_t = sb("xn1_t", [P, G, B * P])[:, :, :]

        h_t = ffn[:, 0:4096].rearrange("p (c t) -> p c t", t=GROUP)
        wup_sb = ffn[:, 4096:6144].rearrange("p (g n) -> p g n", g=G)
        wdown_sb = ffn[:, 6144:7168].rearrange("p (c n) -> p c n", n=P)
        wret_sb = ffn[:, 7168:8192].rearrange("p (c n) -> p c n", n=P)
        hp_t = sb("hp_t", [P, B * P])
        hp = sb("hp", [P, P])
        top_v = sb("top_v", [P, 2 * NH, K])
        top_i = sb("top_i", [P, 2 * NH, K], u32)
        top_f = sb("top_f", [P, 2 * NH, K])
        sums = sb("sums", [P, NH, K, K])
        best = sb("best", [P, NH, K])
        pick = sb("pick", [P, NH, K], u32)
        pick2 = sb("pick2", [P, 2, HK], u32)
        pick2f = sb("pick2f", [P, 2 * HK])
        one_hot = xn1_t.rearrange("p g t -> p (g t)")[:, 0:1024].rearrange("p (a b) -> p a b", b=K)
        chosen = xn1_t.rearrange("p g t -> p (g t)")[:, 1024:2048].rearrange("p (a b) -> p a b", b=K)
        side_i = sb("side_i", [P, 2 * HK])
        expert = sb("expert", [P, HK])
        expert_u = sb("expert_u", [P, HK], u32)
        part_u = sb("part_u", [P, 2, HK], u32)
        lo_bf = sb("lo_bf", [P, HK], bf16)
        by_token = sb("by_token", [P, 3, 2, HK])
        bshift = sb("bshift", [P, NH, K])
        bexp = sb("bexp", [P, NH, K])
        bsum = sb("bsum", [P, NH])
        brec = sb("brec", [P, NH])
        lo_hi_k = sb("lo_hi_k", [P, 2, PAIRS], bf16)
        prob_k = sb("prob_k", [P, PAIRS])
        lo_all = mask_area(0, PAIRS, P)
        pick_r = mask_area(1, PAIRS, P)
        pick_k = mask_area(2, P, PAIRS)
        pick_hi = sb("pick_hi", [P, 2 * EC, PAIRS], bf16)
        z_part = ffn[:, 0:3072].bitcast(bf16).rearrange("p (i t c) -> p i t c", i=3, c=EC)
        z_rest = heads_v[:, 0:1024].rearrange("p (i c t) -> p i c t", i=2, t=P)
        z_sel = heads_v[:, 1024:1536].rearrange("p (i j c) -> p i j c", i=2, c=EC)
        z_k = sb("z_k", [P, PAIRS])
        act_in = sb("act_in", [P, PAIRS])
        act_exp = sb("act_exp", [P, PAIRS])
        act_den = sb("act_den", [P, PAIRS])
        act_rec = sb("act_rec", [P, PAIRS])
        wt = sb("wt", [P, PAIRS])
        wt_rest = sb("wt_rest", [P, PAIRS])
        wt_part = sb("wt_part", [P, 3, PAIRS], bf16)
        wt_hi = ffn[:, 3072:6144].bitcast(bf16).rearrange("p (i c j) -> p i c j", i=3, j=PAIRS)
        wt_e = ffn[:, 6144:8192].rearrange("p (c t) -> p c t", t=P)
        y_out = sb("y_out", [P, D])

        bank = [ps(f"bank{i}", [P, 512]) for i in range(4)]
        wide = ps("wide", [P, 2048])
        bank += [wide[:, i * 512:(i + 1) * 512] for i in range(4)]
        bank = [b[:, :] for b in bank]

        made = {}

        def s(name):
            if name not in made:
                made[name] = ctx.enter_context(nc.semaphore(name))
            return made[name]

        def reuse(eng, name, count):
            if not isinstance(count, int) or count > 0:
                eng.wait_ge(s(name), count)

        def wait_apart(eng, name):
            eng.sem_inc(s(name), 1)

        class Chain:
            def __init__(self, eng, name):
                self.eng, self.sem, self.base, self.n = eng, s(name), 0, 0

            def link(self, ins):
                self.n += 1
                ins.then_inc(self.sem, 1)
                self.eng.wait_ge(self.sem, self.base + self.n)

        def tiles(eng, body, chain=None):
            n0 = chain.n if chain else 0
            body(0)
            steps = chain.n - n0 if chain else 0
            if chain:
                before = chain.base + chain.n
            with eng.Fori(1, B - 1) as t:
                if chain:
                    chain.base, chain.n = t * steps + (before - steps), 0
                body(t)
                assert not chain or chain.n == steps
            if chain:
                chain.base, chain.n = before + (B - 2) * steps, 0

        sides = ((0, 0, MAIN), (1, MAIN, KEYS))
        block = ctx.enter_context(nc.Block())

        @block.sync
        def _(sp):
            def load_y(t):
                reuse(sp, "qkv_ps", t)
                sp.dma_start(y_main[:, 0:MAIN], y_t[bass.ds(t, 1), :, 0:MAIN].rearrange("a p n -> (a p) n")).then_inc(s("y_in"), 16)
                sp.dma_start(y_dca[:, MAIN:P], y_t[bass.ds(t, 1), :, MAIN:P].rearrange("a p n -> (a p) n")).then_inc(s("y_in"), 16)

            sp.dma_start(x_sb[:, :, :], x.rearrange("b p n -> p b n")).then_inc(s("x_in"), 16)
            sp.dma_start(wq_sb[:, :, :], w_q.rearrange("(g p) n -> p g n", p=P)).then_inc(s("wqkv_in"), 16)
            sp.dma_start(wkv_sb[:, :, :], w_kv.rearrange("a p n -> p a n")).then_inc(s("wqkv_in"), 16)
            sp.dma_start(bqkv[:, 0:D], b_q.unsqueeze(0).broadcast_to([P, D])).then_inc(s("wqkv_in"), 16)
            sp.dma_start(bqkv[0:MAIN, D:3 * D], b_kv[0:1, :].broadcast_to([MAIN, 2 * D])).then_inc(s("wqkv_in"), 16)
            sp.dma_start(bqkv[MAIN:P, D:3 * D], b_kv[1:2, :].broadcast_to([DCA, 2 * D])).then_inc(s("wqkv_in"), 16)
            sp.dma_start(gate_in[:, :], gates.unsqueeze(0).broadcast_to([P, 2])).then_inc(s("gate_in"), 16)
            sp.dma_start(bo_t[:, :], b_o.unsqueeze(0).broadcast_to([P, D])).then_inc(s("gate_in"), 16)
            sp.dma_start(wb[:, :], ln_wb).then_inc(s("wb_in"), 16)
            sp.wait_ge(s("y_zero"), 2)
            load_y(0)
            sp.dma_start(wo_sb[:, :, :], w_o.rearrange("(g p) n -> p g n", p=P)).then_inc(s("wo_in"), 16)
            sp.dma_start(wup_sb[:, :, :], w_up_t.rearrange("(g p) n -> p g n", p=P)).then_inc(s("ffn_in"), 16)
            sp.dma_start(bup_sb[:, :], b_up).then_inc(s("ffn_in"), 16)
            sp.dma_start(wdown_sb[:, :, :], w_down_t.rearrange("(c p) n -> p c n", p=P)).then_inc(s("ffn_in"), 16)
            sp.dma_start(bdown_sb[:, :], b_down).then_inc(s("ffn_in"), 16)
            sp.dma_start(wret_sb[:, :, :], w_ret.rearrange("(c p) n -> p c n", p=P)).then_inc(s("ret_in"), 16)
            sp.dma_start(keys_sb[:, :, :], keys_t).then_inc(s("ret_in"), 16)
            sp.dma_start(down_sb[:, :, :], down_t.rearrange("p (c r) -> p c r", r=P)).then_inc(s("ret_in"), 16)
            sp.dma_start(up_sb[:, :, :], up.rearrange("(c r) n -> r c n", r=P)).then_inc(s("ret_in"), 16)
            with sp.Fori(1, B) as t:
                load_y(t)

            def spread_lo(t):
                row = lo_scratch[bass.ds(t, 1)]
                sp.wait_ge(s("lo_ready"), t + 1)
                for side in range(2):
                    sp.dma_start(row[:, :, side, :].rearrange("a j k -> (a j) k"),
                                 lo_bf[side * PAIRS:(side + 1) * PAIRS, :]).then_inc(s("lo_stored"), 16)
                sp.wait_ge(s("lo_stored"), (t + 1) * 32)
                reuse(sp, "pick_r_ready", t)
                sp.dma_start(lo_all[:, :, :].rearrange("p a b -> p (a b)"),
                             row.rearrange("a j s k -> a (j s k)").broadcast_to([P, PAIRS * P])).then_inc(s("lo_all_in"), 16)

            def store(t):
                sp.wait_ge(s("y_ready"), t + 1)
                sp.dma_start(out[bass.ds(t, 1)].rearrange("a p n -> (a p) n"), y_out[:, :]).then_inc(s("y_stored"), 16)

            def both(t):
                spread_lo(t + 1)
                store(t)

            spread_lo(0)
            tiles(sp, both)
            store(B - 1)
            sp.wait_ge(s("y_stored"), 16 * B)

        @block.gpsimd
        def _(pool):
            chain = Chain(pool, "pool_step")
            link = chain.link
            pool.memset(y_main[:, :], 0.0).then_inc(s("y_zero"), 1)
            pool.memset(y_dca[:, :], 0.0).then_inc(s("y_zero"), 1)
            link(pool.memset(minus_half[:, :], -0.5))
            link(pool.memset(ident[:, :], 0.0))
            pool.affine_select(out=ident[:, :], in_=ident[:, :], compare_op=ALU.not_equal, fill=1.0, base=0,
                               pattern=[[-1, P]], channel_multiplier=1).then_inc(s("ident_ready"), 1)
            link(pool.memset(head_mask[:, :], 1.0))
            link(pool.affine_select(out=head_mask[:, :], in_=head_mask[:, :], compare_op=ALU.is_ge, fill=0.0,
                                    base=0, pattern=[[-HD, HG]], channel_multiplier=1))
            link(pool.affine_select(out=head_mask[:, :], in_=head_mask[:, :], compare_op=ALU.is_ge, fill=0.0,
                                    base=HD - 1, pattern=[[HD, HG]], channel_multiplier=-1))
            link(pool.memset(v_diag[:, :, :], 0.0))
            pool.wait_ge(s("xvar_ready"), 1)
            pool.tensor_tensor(xrstd[:, :], xvar[:, :], minus_half[:, 0:B], ALU.pow).then_inc(s("xrstd_ready"), 1)

            pool.wait_ge(s("bo_ready"), 1)
            pool.tensor_tensor(x1[:, :, :], x_sb[:, :, :], bo_t[:, :].unsqueeze(1).broadcast_to([P, B, D]), ALU.add).then_inc(s("x1_ready"), 1)

            def rstd_qk(t):
                pool.wait_ge(s("qk_var_ready"), t + 1)
                reuse(pool, "qkn_ready", t)
                pool.tensor_tensor(qk_rstd[:, :], qk_var[:, :], minus_half[:, :], ALU.pow).then_inc(s("qk_rstd_ready"), 1)

            def normalise(t):
                for g in range(G):
                    hs = slice(g * HG, (g + 1) * HG)
                    pool.wait_ge(s("rsum_ready"), G * t + g + 1)
                    reuse(pool, "prob_t_ps", G * t + (g + 1 - G))
                    for side, c0, c1 in sides:
                        last = pool.tensor_tensor(pnorm[:, hs, c0:c1], prob[:, hs, c0:c1],
                                                  rsum[:, side, hs].unsqueeze(2).broadcast_to([P, HG, c1 - c0]), ALU.mult)
                    last.then_inc(s("pnorm_ready"), 1)

            def diagonals(t):
                pool.wait_ge(s("k_t_ready"), 2 * (t + 1))
                reuse(pool, "scores_ready", G * t)
                for g in range(G):
                    last = pool.tensor_tensor(k_diag[:, g, :, :], k_t[:, g, :].unsqueeze(1).broadcast_to([P, HG, P]),
                                              head_mask[:, :].unsqueeze(2).broadcast_to([P, HG, P]), ALU.mult)
                last.then_inc(s("k_diag_ready"), 1)

            def v_place(t):
                pool.wait_ge(s("v_ready"), t + 1)
                reuse(pool, "ctx_ps", t)
                wait_apart(pool, "pool_passed")
                pool.tensor_copy(v_diag[:, :, :].rearrange("p g (h c) -> p (g h) c", c=P + HD)[:, :, 0:HD],
                                 v_sb[:, :].rearrange("p (h d) -> p h d", d=HD)).then_inc(s("v_diag_ready"), 1)

            def rstd_x1(t):
                pool.wait_ge(s("var1_ready"), t + 1)
                reuse(pool, "xn1_ready", t)
                pool.tensor_tensor(rstd1[:, :], var1[:, :], minus_half[:, 0:1], ALU.pow).then_inc(s("rstd1_ready"), 1)

            def attention(t):
                rstd_qk(t + 1)
                normalise(t)
                diagonals(t + 1)
                rstd_x1(t)
                v_place(t + 1)

            rstd_qk(0)
            diagonals(0)
            v_place(0)
            tiles(pool, attention)
            normalise(B - 1)
            rstd_x1(B - 1)

            pool.iota(iota_p[:, :], pattern=[[0, 1]], base=0, channel_multiplier=1, allow_small_or_imprecise_dtypes=True)
            pool.iota(iota8[:, :], pattern=[[1, K]], base=0, channel_multiplier=0, allow_small_or_imprecise_dtypes=True)
            pool.iota(iota_hi[:, :, :], pattern=[[1, 2 * EC], [0, PAIRS]], base=0, channel_multiplier=0, allow_small_or_imprecise_dtypes=True)
            pool.iota(iota_lo[:, :, :], pattern=[[1, P], [0, PAIRS]], base=0, channel_multiplier=0,
                      allow_small_or_imprecise_dtypes=True).then_inc(s("iota_ready"), 1)

            def z_low(t):
                for q in range(4):
                    pool.wait_ge(s("z_mid_ready"), 4 * t + q + 1)
                    pool.tensor_tensor(z_part[:, 2, :, 4 * q:4 * q + 4].rearrange("p t c -> p c t"), z_rest[:, q % 2, :, :],
                                       z_part[:, 1, :, 4 * q:4 * q + 4].rearrange("p t c -> p c t"),
                                       ALU.subtract).then_inc(s("z_low_ready"), 1)

            with pool.Fori(0, B) as t:
                z_low(t)

        @block.scalar
        def _(act):
            act.wait_ge(s("gate_in"), 32)
            act.activation(gate[:, :], gate_in[:, :], ACT.Tanh).then_inc(s("gate_ready"), 1)
            act.wait_ge(s("wb_in"), 16)

            def take_xn(t):
                act.wait_ge(s("xn_t_ps"), t + 1)
                reuse(act, "qkv_ps", t)
                act.activation(xn_t[:, :, :].rearrange("p g c -> p (g c)"), bank[0][:, 0:D], ACT.Copy).then_inc(s("xn_t_ready"), 1)

            def squares(t):
                act.wait_ge(s("qk_ready"), t + 1)
                reuse(act, "qk_ss_ready", t)
                act.activation(qk_sq[:, :, :], qk[:, :, :], ACT.Square).then_inc(s("qk_sq_ready"), 1)

            def take_qk(t):
                tq = bank[3][:, 0:D].rearrange("p (g c) -> p g c", c=P)
                tk = bank[3][:, D:2 * D].rearrange("p (g c) -> p g c", c=P)
                act.wait_ge(s("qk_t_ps"), t + 1)
                reuse(act, "scores_ready", G * t)
                act.activation(q_t[:, :, :], tq, ACT.Identity, scale=wb[:, 0:1], bias=wb[:, 1:2]).then_inc(s("q_t_ready"), 1)
                reuse(act, "k_diag_ready", t)
                act.activation(k_t[:, :, 0:MAIN], tk[:, :, 0:MAIN], ACT.Identity, scale=wb[:, 2:3], bias=wb[:, 3:4]).then_inc(s("k_t_ready"), 1)
                act.activation(k_t[:, :, MAIN:P], tk[:, :, MAIN:P], ACT.Identity, scale=wb[:, 4:5], bias=wb[:, 5:6]).then_inc(s("k_t_ready"), 1)

            def exps(t):
                for g in range(G):
                    hs = slice(g * HG, (g + 1) * HG)
                    act.wait_ge(s("shifted_ready"), G * t + g + 1)
                    reuse(act, "pnorm_ready", G * t + (g + 1 - G))
                    act.activation(prob[:, hs, :], shifted[:, hs, :], ACT.Exp, scale=SCALE).then_inc(s("prob_ready"), 1)

            def take_prob(t):
                for g in range(G):
                    hs = slice(g * HG, (g + 1) * HG)
                    act.wait_ge(s("prob_t_ps"), G * t + g + 1)
                    reuse(act, "ctx_ps", t)
                    act.activation(prob_t[:, hs, :].rearrange("p h c -> p (h c)"), wide[:, g * HG * P:(g + 1) * HG * P],
                                   ACT.Copy).then_inc(s("prob_t_ready"), 1)

            def take_ctx(t):
                act.wait_ge(s("ctx_ps"), t + 1)
                reuse(act, "attn_ps", t)
                act.activation(ctx_t[:, :, :].rearrange("p g c -> p (g c)"), bank[4][:, 0:D], ACT.Copy).then_inc(s("ctx_t_ready"), 1)

            def take_xn1(t):
                act.wait_ge(s("xn1_t_ps"), t + 1)
                act.activation(xn1_t[:, :, bass.ds(t * P, P)], bank[3][:, 0:D].rearrange("p (g c) -> p g c", c=P),
                               ACT.Copy).then_inc(s("xn1_t_ready"), 1)

            def attention(t):
                exps(t)
                take_xn(t + 1)
                squares(t + 1)
                take_prob(t)
                take_qk(t + 1)
                take_ctx(t)
                take_xn1(t)

            take_xn(0)
            squares(0)
            take_qk(0)
            tiles(act, attention)
            exps(B - 1)
            take_prob(B - 1)
            take_ctx(B - 1)
            take_xn1(B - 1)

            act.wait_ge(s("ffn_in"), 64)
            act.wait_ge(s("simw_ps"), 2)
            for side in range(2):
                for odd in range(2):
                    act.activation(simw[:, side * NH * NK:(side + 1) * NH * NK].rearrange("p (h o k) -> p h o k", o=2, k=NK)[:, :, odd, :],
                                   bank[3 + side + 2 * odd][:, 0:NH // 2 * NK].rearrange("p (h k) -> p h k", k=NK), ACT.Copy).then_inc(s("simw_ready"), 1)
            for g in range(B * P // GROUP):
                reuse(act, "down_ps", g)
                for c in range(NC):
                    act.wait_ge(s("up_ps"), g * NC + c + 1)
                    act.activation(h_t[:, c, :], bank[c % 2], ACT.Silu, bias=bup_sb[:, c:c + 1]).then_inc(s("h_t_ready"), 1)
                act.wait_ge(s("down_ps"), g + 1)
                act.activation(hp_t[:, g * GROUP:(g + 1) * GROUP], bank[2], ACT.Identity, bias=bdown_sb[:, 0:1]).then_inc(s("hp_t_ready"), 1)
            act.wait_ge(s("hp_t_ready"), B * P // GROUP)

            def take_hp(t):
                reuse(act, "z_ps", 4 * t)
                act.activation(hp[:, :], hp_t[:, bass.ds(t * P, P)], ACT.Copy).then_inc(s("hp_ready"), 1)

            def split_z(t):
                reuse(act, "z_sel_ps", 4 * t)
                for q in range(4):
                    act.wait_ge(s("z_ps"), 4 * t + q + 1)
                    act.activation(z_part[:, 0, :, 4 * q:4 * q + 4].rearrange("p t c -> p c t"),
                                   bank[3 + q % 2].rearrange("p (c t) -> p c t", t=P), ACT.Copy).then_inc(s("z_top_ready"), 1)
                    act.wait_ge(s("z_rest_ready"), 4 * t + q + 1)
                    act.activation(z_part[:, 1, :, 4 * q:4 * q + 4].rearrange("p t c -> p c t"), z_rest[:, q % 2, :, :],
                                   ACT.Copy).then_inc(s("z_mid_ready"), 1)

            def exp_best(t):
                act.wait_ge(s("bshift_ready"), t + 1)
                reuse(act, "by_token_ready", t)
                act.activation(bexp[:, :, :], bshift[:, :, :], ACT.Exp).then_inc(s("bexp_ready"), 1)

            def take_by_k(t):
                act.wait_ge(s("by_k_ps"), t + 1)
                reuse(act, "pick_k_ready", t)
                reuse(act, "act_in_ready", t)
                for side in range(2):
                    rows = slice(side * PAIRS, (side + 1) * PAIRS)
                    src = bank[2].rearrange("p (i t) -> p i t", t=P)[rows, :, side * PAIRS:(side + 1) * PAIRS]
                    act.activation(lo_hi_k[rows, :, :], src[:, 0:2, :], ACT.Copy).then_inc(s("by_k_ready"), 1)
                    act.activation(prob_k[rows, :], src[:, 2, :], ACT.Copy).then_inc(s("by_k_ready"), 1)

            def exp_act(t):
                act.wait_ge(s("act_in_ready"), t + 1)
                reuse(act, "wt_hi_ready", t)
                act.activation(act_exp[:, :], act_in[:, :], ACT.Exp, scale=-1.0).then_inc(s("act_exp_ready"), 1)

            def take_wt(t):
                reuse(act, "out_ps", t)
                for q in range(4):
                    act.wait_ge(s("wt_e_ps"), 4 * t + q + 1)
                    for side in range(2):
                        act.activation(
                            wt_e[:, :, side * PAIRS + q * QP:side * PAIRS + (q + 1) * QP].rearrange("p c j -> p j c"),
                            bank[5 + q % 2].rearrange("p (j s c) -> p j s c", s=2, c=EC)[:, :, side, :],
                            ACT.Copy).then_inc(s("wt_e_ready"), 1)

            def experts(t):
                take_hp(t + 1)
                exp_act(t)
                split_z(t + 1)
                take_wt(t)
                exp_best(t + 1)
                take_by_k(t + 1)

            take_hp(0)
            split_z(0)
            exp_best(0)
            take_by_k(0)
            tiles(act, experts)
            exp_act(B - 1)
            take_wt(B - 1)

        @block.vector
        def _(dve):
            chain = Chain(dve, "dve_step")
            link = chain.link

            dve.wait_ge(s("wqkv_in"), 80)
            tensors = [wq_sb[:, 0, :], wq_sb[:, 1, :], wkv_sb[:, 0, 0:D], wkv_sb[:, 1, 0:D], bqkv[:, 0:D], bqkv[:, D:2 * D]]
            tensors = [a.rearrange("p (h d) -> p h d", d=HD) for a in tensors]
            for i, a in enumerate(tensors):
                last = dve.tensor_reduce(means[:, i, :], a, X, ALU.add)
            link(last)
            link(dve.tensor_scalar(means[:, :, :], means[:, :, :], 1.0 / HD, None, ALU.mult))
            for i, a in enumerate(tensors):
                last = dve.tensor_tensor(a, a, means[:, i, :].unsqueeze(2).broadcast_to([P, H, HD]), ALU.subtract)
            last.then_inc(s("wqk_ready"), 1)
            dve.wait_ge(s("wqk_ready"), 1)
            dve.wait_ge(s("x_in"), 16)
            for t in range(B):
                last = dve.bn_stats(xstat[:, t, :], x_sb[:, t, :])
            link(last)
            for t in range(B):
                last = dve.bn_aggr(xmv[:, t, :], xstat[:, t, :])
            link(last)
            dve.tensor_scalar(xvar[:, :], xmv[:, :, 1], EPS_X, None, ALU.add).then_inc(s("xvar_ready"), 1)
            dve.wait_ge(s("gate_ready"), 1)
            dve.tensor_scalar(bo_t[:, :], bo_t[:, :], gate[:, 0:1], None, ALU.mult).then_inc(s("bo_ready"), 1)

            def norm_x(t):
                reuse(dve, "xn_t_ps", t)
                dve.tensor_scalar(xn[:, :].unsqueeze(1), x_sb[:, bass.ds(t, 1), :], xmv[:, bass.ds(t, 1), 0], xrstd[:, bass.ds(t, 1)],
                                  ALU.subtract, ALU.mult).then_inc(s("xn_ready"), 1)

            def bias_qkv(t):
                dve.wait_ge(s("qkv_ps"), t + 1)
                reuse(dve, "qkn_ready", t)
                dve.tensor_tensor(qk[:, :, :].rearrange("p h d -> p (h d)"), bank[1], bqkv[:, 0:2 * D], ALU.add).then_inc(s("qk_ready"), 1)
                reuse(dve, "v_diag_ready", t)
                dve.tensor_tensor(v_sb[:, :], bank[2][:, 0:D], bqkv[:, 2 * D:3 * D], ALU.add).then_inc(s("v_ready"), 1)

            def var_qk(t):
                dve.wait_ge(s("qk_sq_ready"), t + 1)
                dve.tensor_reduce(qk_ss[:, :], qk_sq[:, :, :], X, ALU.add).then_inc(s("qk_ss_ready"), 1)
                dve.wait_ge(s("qk_ss_ready"), t + 1)
                dve.tensor_scalar(qk_var[:, :], qk_ss[:, :], 1.0 / HD, EPS_QK, ALU.mult, ALU.add).then_inc(s("qk_var_ready"), 1)

            def norm_qk(t):
                dve.wait_ge(s("qk_rstd_ready"), t + 1)
                reuse(dve, "qk_t_ps", t)
                dve.tensor_tensor(qkn[:, :, :], qk[:, :, :], qk_rstd[:, :].unsqueeze(2).broadcast_to([P, 2 * H, HD]),
                                  ALU.mult).then_inc(s("qkn_ready"), 1)

            def softmax_shift(t):
                for g in range(G):
                    hs = slice(g * HG, (g + 1) * HG)
                    sc = wide[:, g * HG * P:(g + 1) * HG * P].rearrange("p (h k) -> p h k", k=KEYS)
                    dve.wait_ge(s("scores_ready"), G * t + g + 1)
                    for side, c0, c1 in sides:
                        last = dve.tensor_reduce(smax[:, side, hs], sc[:, :, c0:c1], X, ALU.max)
                    link(last)
                    reuse(dve, "prob_ready", G * t + (g + 1 - G))
                    for side, c0, c1 in sides:
                        last = dve.tensor_tensor(shifted[:, hs, c0:c1], sc[:, :, c0:c1],
                                                 smax[:, side, hs].unsqueeze(2).broadcast_to([P, HG, c1 - c0]), ALU.subtract)
                    last.then_inc(s("shifted_ready"), 1)

            def softmax_sum(t):
                for g in range(G):
                    hs = slice(g * HG, (g + 1) * HG)
                    dve.wait_ge(s("prob_ready"), G * t + g + 1)
                    for side, c0, c1 in sides:
                        last = dve.tensor_reduce(ssum[:, side, hs], prob[:, hs, c0:c1], X, ALU.add)
                    link(last)
                    reuse(dve, "pnorm_ready", G * t + (g + 1 - G))
                    dve.reciprocal(rsum[:, :, hs], ssum[:, :, hs]).then_inc(s("rsum_ready"), 1)

            def residual(t):
                row = x1[:, bass.ds(t, 1), :]
                dve.wait_ge(s("attn_ps"), t + 1)
                dve.scalar_tensor_tensor(row, bank[0][:, 0:D].unsqueeze(1), gate[:, 0:1], row, ALU.mult, ALU.add).then_inc(s("x1_done"), 1)
                dve.wait_ge(s("x1_done"), t + 1)
                wait_apart(dve, "dve_passed")
                link(dve.bn_stats(stat1[:, :], row.rearrange("p a n -> p (a n)")))
                wait_apart(dve, "dve_passed")
                link(dve.bn_aggr(mv1[:, :], stat1[:, :]))
                reuse(dve, "rstd1_ready", t)
                dve.tensor_scalar(var1[:, :], mv1[:, 1:2], EPS_X, None, ALU.add).then_inc(s("var1_ready"), 1)
                dve.wait_ge(s("rstd1_ready"), t + 1)
                reuse(dve, "xn1_t_ps", t)
                dve.tensor_scalar(xn1[:, :].unsqueeze(1), row, mv1[:, 0:1], rstd1[:, :], ALU.subtract, ALU.mult).then_inc(s("xn1_ready"), 1)

            def attention(t):
                norm_x(t + 1)
                softmax_shift(t)
                bias_qkv(t + 1)
                var_qk(t + 1)
                softmax_sum(t)
                norm_qk(t + 1)
                residual(t)

            dve.wait_ge(s("xrstd_ready"), 1)
            norm_x(0)
            bias_qkv(0)
            var_qk(0)
            norm_qk(0)
            dve.wait_ge(s("x1_ready"), 1)
            tiles(dve, attention, chain)
            softmax_shift(B - 1)
            softmax_sum(B - 1)
            residual(B - 1)

            def top_keys(t):
                dve.wait_ge(s("sim_ps"), t + 1)
                wait_apart(dve, "dve_passed")
                sims = [bank[side][:, h * NK:(h + 1) * NK] for side in range(2) for h in range(NH)]
                for i, sim in enumerate(sims):
                    last = dve.max(top_v[:, i, :], sim)
                link(last)
                wait_apart(dve, "dve_passed")
                for i, sim in enumerate(sims):
                    last = dve.max_index(top_i[:, i, :], top_v[:, i, :], sim)
                last.then_inc(s("top_ready"), 1)
                dve.tensor_tensor(sums[:, :, :, :], top_v[:, 0:NH, :].unsqueeze(3).broadcast_to([P, NH, K, K]),
                                  top_v[:, NH:2 * NH, :].unsqueeze(2).broadcast_to([P, NH, K, K]), ALU.add)
                dve.wait_ge(s("top_ready"), t + 1)
                link(dve.tensor_copy(top_f[:, :, :], top_i[:, :, :]))
                wait_apart(dve, "dve_passed")

            def top_experts(t):
                for h in range(NH):
                    last = dve.max(best[:, h, :], sums[:, h, :, :].rearrange("p a b -> p (a b)"))
                link(last)
                dve.tensor_tensor(bshift[:, :, :], best[:, :, :], best[:, :, 0:1].broadcast_to([P, NH, K]), ALU.subtract).then_inc(s("bshift_ready"), 1)
                for h in range(NH):
                    last = dve.max_index(pick[:, h, :], best[:, h, :], sums[:, h, :, :].rearrange("p a b -> p (a b)"))
                link(last)
                flat = pick[:, :, :].rearrange("p h k -> p (h k)")
                dve.tensor_scalar(pick2[:, 0, :], flat, 3, None, ALU.logical_shift_right)
                link(dve.tensor_scalar(pick2[:, 1, :], flat, K - 1, None, ALU.bitwise_and))
                link(dve.tensor_copy(pick2f[:, :], pick2[:, :, :].rearrange("p s k -> p (s k)")))
                link(dve.tensor_tensor(one_hot[:, :, :], pick2f[:, :].unsqueeze(2).broadcast_to([P, 2 * HK, K]),
                                       iota8[:, :].unsqueeze(1).broadcast_to([P, 2 * HK, K]), ALU.is_equal))
                link(dve.tensor_tensor(chosen[:, :, :].rearrange("p (g k) a -> p g k a", k=K), one_hot[:, :, :].rearrange("p (g k) a -> p g k a", k=K),
                                       top_f[:, :, :].unsqueeze(2).broadcast_to([P, 2 * NH, K, K]), ALU.mult))
                link(dve.tensor_reduce(side_i[:, :], chosen[:, :, :], X, ALU.add))
                link(dve.scalar_tensor_tensor(expert_u[:, :], side_i[:, 0:HK], float(NK), side_i[:, HK:2 * HK], ALU.mult, ALU.add))
                dve.tensor_scalar(part_u[:, 0, :], expert_u[:, :], P - 1, None, ALU.bitwise_and)
                link(dve.tensor_scalar(part_u[:, 1, :], expert_u[:, :], 7, None, ALU.logical_shift_right))
                reuse(dve, "lo_stored", 32 * t)
                dve.tensor_copy(lo_bf[:, :], part_u[:, 0, :]).then_inc(s("lo_ready"), 1)
                reuse(dve, "by_k_ps", t)
                dve.tensor_copy(by_token[:, 0, :, :], part_u[:, 0:1, :].broadcast_to([P, 2, HK]))
                dve.tensor_copy(by_token[:, 1, 0, :], part_u[:, 1, :])
                dve.tensor_scalar(by_token[:, 1, 1, :], part_u[:, 1, :], float(EC), None, ALU.add)
                dve.wait_ge(s("bexp_ready"), t + 1)
                link(dve.tensor_reduce(bsum[:, :], bexp[:, :, :], X, ALU.add))
                link(dve.reciprocal(brec[:, :], bsum[:, :]))
                for side in range(2):
                    last = dve.tensor_tensor(by_token[:, 2, side, :].rearrange("p (h k) -> p h k", k=K), bexp[:, :, :],
                                             brec[:, :].unsqueeze(2).broadcast_to([P, NH, K]), ALU.mult)
                last.then_inc(s("by_token_ready"), 1)

            def rest_z(t):
                for q in range(4):
                    dve.wait_ge(s("z_top_ready"), 4 * t + q + 1)
                    reuse(dve, "z_low_ready", 4 * t + (q - 1))
                    dve.tensor_tensor(z_rest[:, q % 2, :, :], bank[3 + q % 2].rearrange("p (c t) -> p c t", t=P),
                                      z_part[:, 0, :, 4 * q:4 * q + 4].rearrange("p t c -> p c t"), ALU.subtract).then_inc(s("z_rest_ready"), 1)

            def masks(t):
                dve.wait_ge(s("lo_all_in"), 16 * (t + 1))
                reuse(dve, "z_sel_ps", 4 * t)
                dve.tensor_scalar(pick_r[:, :, :], lo_all[:, :, :], iota_p[:, 0:1], None, ALU.is_equal).then_inc(s("pick_r_ready"), 1)
                dve.wait_ge(s("by_k_ready"), 4 * (t + 1))
                reuse(dve, "wt_hi_ready", t)
                reuse(dve, "wt_e_ps", 4 * t)
                dve.tensor_tensor(pick_hi[:, :, :], lo_hi_k[:, 1:2, :].broadcast_to([P, 2 * EC, PAIRS]), iota_hi[:, :, :], ALU.is_equal)
                dve.tensor_tensor(pick_k[:, :, :], lo_hi_k[:, 0:1, :].broadcast_to([P, P, PAIRS]), iota_lo[:, :, :],
                                  ALU.is_equal).then_inc(s("pick_k_ready"), 1)

            def select_z(t):
                dve.wait_ge(s("pick_k_ready"), t + 1)
                for q in range(4):
                    dve.wait_ge(s("z_sel_ps"), 4 * t + q + 1)
                    for side in range(2):
                        rows = slice(side * PAIRS, (side + 1) * PAIRS)
                        last = dve.tensor_tensor(z_sel[rows, q % 2, :, :],
                                                 bank[5 + q % 2].rearrange("p (j s c) -> p j s c", s=2, c=EC)[rows, :, side, :],
                                                 pick_hi[rows, side * EC:(side + 1) * EC, q * QP:(q + 1) * QP].rearrange("p c j -> p j c"), ALU.mult)
                    last.then_inc(s("z_sel_read"), 1)
                    dve.wait_ge(s("z_sel_read"), 4 * t + q + 1)
                    last = dve.tensor_reduce(z_k[:, q * QP:(q + 1) * QP], z_sel[:, q % 2, :, :], X, ALU.add)
                link(last)
                dve.tensor_tensor(act_in[:, :], z_k[:, :], prob_k[:, :], ALU.mult).then_inc(s("act_in_ready"), 1)

            def weights(t):
                dve.wait_ge(s("act_exp_ready"), t + 1)
                link(dve.tensor_scalar(act_den[:, :], act_exp[:, :], 1.0, None, ALU.add))
                link(dve.reciprocal(act_rec[:, :], act_den[:, :]))
                link(dve.tensor_tensor(wt[:, :], act_in[:, :], act_rec[:, :], ALU.mult))
                link(dve.tensor_copy(wt_part[:, 0, :], wt[:, :]))
                link(dve.tensor_tensor(wt_rest[:, :], wt[:, :], wt_part[:, 0, :], ALU.subtract))
                link(dve.tensor_copy(wt_part[:, 1, :], wt_rest[:, :]))
                link(dve.tensor_tensor(wt_part[:, 2, :], wt_rest[:, :], wt_part[:, 1, :], ALU.subtract))
                reuse(dve, "wt_e_ps", 4 * t)
                for part in range(3):
                    last = dve.tensor_tensor(wt_hi[:, part, :, :], pick_hi[:, :, :],
                                             wt_part[:, part:part + 1, :].broadcast_to([P, 2 * EC, PAIRS]), ALU.mult)
                last.then_inc(s("wt_hi_ready"), 1)

            def finish(t):
                dve.wait_ge(s("out_ps"), t + 1)
                reuse(dve, "y_stored", 16 * t)
                dve.scalar_tensor_tensor(y_out[:, :].unsqueeze(1), bank[7][:, 0:D].unsqueeze(1), gate[:, 1:2], x1[:, bass.ds(t, 1), :],
                                         ALU.mult, ALU.add).then_inc(s("y_ready"), 1)

            def experts(t):
                select_z(t)
                weights(t)
                rest_z(t + 1)
                top_keys(t + 1)
                top_experts(t + 1)
                finish(t)
                masks(t + 1)

            dve.wait_ge(s("iota_ready"), 1)
            rest_z(0)
            top_keys(0)
            top_experts(0)
            masks(0)
            tiles(dve, experts, chain)
            select_z(B - 1)
            weights(B - 1)
            finish(B - 1)

        @block.tensor
        def _(pe):
            mm = pe.matmul

            def transpose(to, what):
                return pe.transpose(to, what, ident[:, :])

            def turn_xn(t):
                pe.wait_ge(s("xn_ready"), t + 1)
                reuse(pe, "x1_done", t - 1)
                for g in range(G):
                    last = transpose(bank[0][:, g * P:(g + 1) * P], xn[:, g * P:(g + 1) * P])
                last.then_inc(s("xn_t_ps"), 1)

            def qkv(t):
                pe.wait_ge(s("xn_t_ready"), t + 1)
                reuse(pe, "v_ready", t)
                for g in range(G):
                    mm(bank[1][:, 0:D], xn_t[:, g, :], wq_sb[:, g, :], start=g == 0, stop=g == G - 1)
                pe.wait_ge(s("y_in"), 32 * (t + 1))
                for i, to in enumerate((bank[1][:, D:2 * D], bank[2][:, 0:D])):
                    cols = slice(i * D, (i + 1) * D)
                    mm(to, y_main[:, :], wkv_sb[:, 0, cols], start=True, stop=False)
                    last = mm(to, y_dca[:, :], wkv_sb[:, 1, cols], start=False, stop=True)
                last.then_inc(s("qkv_ps"), 1)

            def turn_qk(t):
                flat = qkn[:, :, :].rearrange("p h d -> p (h d)")
                pe.wait_ge(s("qkn_ready"), t + 1)
                reuse(pe, "xn1_t_ready", t - 1)
                for i in range(2 * G):
                    last = transpose(bank[3][:, i * P:(i + 1) * P], flat[:, i * P:(i + 1) * P])
                last.then_inc(s("qk_t_ps"), 1)

            def scores(t):
                pe.wait_ge(s("q_t_ready"), t + 1)
                pe.wait_ge(s("k_diag_ready"), t + 1)
                reuse(pe, "ctx_t_ready", t)
                for g in range(G):
                    for half in range(2):
                        last = mm(bank[4 + 2 * g + half], q_t[:, g, :],
                                  k_diag[:, g, half * HG // 2:(half + 1) * HG // 2, :].rearrange("p h c -> p (h c)"), start=True, stop=True)
                    last.then_inc(s("scores_ready"), 1)

            def turn_prob(t):
                for g in range(G):
                    pe.wait_ge(s("pnorm_ready"), G * t + g + 1)
                    for h in range(g * HG, (g + 1) * HG):
                        last = transpose(wide[:, h * P:(h + 1) * P], pnorm[:, h, :])
                    last.then_inc(s("prob_t_ps"), 1)

            def context(t):
                pe.wait_ge(s("v_diag_ready"), t + 1)
                for g in range(G):
                    pe.wait_ge(s("prob_t_ready"), G * t + g + 1)
                    for h in range(HG):
                        last = mm(bank[4][:, g * P:(g + 1) * P], v_diag[:, g, h * P:(h + 1) * P], prob_t[:, g * HG + h, :],
                                  start=h == 0, stop=h == HG - 1)
                last.then_inc(s("ctx_ps"), 1)
                pe.wait_ge(s("ctx_t_ready"), t + 1)
                for g in range(G):
                    last = mm(bank[0][:, 0:D], ctx_t[:, g, :], wo_sb[:, g, :], start=g == 0, stop=g == G - 1)
                last.then_inc(s("attn_ps"), 1)

            def turn_xn1(t):
                pe.wait_ge(s("xn1_ready"), t + 1)
                pe.wait_ge(s("k_t_ready"), 2 * min(t + 2, B) if isinstance(t, int) else 2 * (t + 2))
                for g in range(G):
                    last = transpose(bank[3][:, g * P:(g + 1) * P], xn1[:, g * P:(g + 1) * P])
                last.then_inc(s("xn1_t_ps"), 1)

            def attention(t):
                scores(t)
                turn_xn(t + 1)
                qkv(t + 1)
                turn_prob(t)
                turn_qk(t + 1)
                context(t)
                turn_xn1(t)

            pe.wait_ge(s("ident_ready"), 1)
            pe.wait_ge(s("wqk_ready"), 1)
            turn_xn(0)
            qkv(0)
            turn_qk(0)
            pe.wait_ge(s("wo_in"), 16)
            tiles(pe, attention)
            scores(B - 1)
            turn_prob(B - 1)
            context(B - 1)
            turn_xn1(B - 1)

            pe.wait_ge(s("ret_in"), 64)
            pe.wait_ge(s("xn1_t_ready"), B)
            for i in range(2 * NH):
                rows = slice(i % 2 * (P // 2), (i % 2 + 1) * (P // 2))
                h = i % NH // 2
                last = mm(bank[3 + i // NH + i % 2 * 2][:, h * NK:(h + 1) * NK], wret_sb[rows, i // 2, :], keys_sb[rows, i // 2, :], start=True, stop=True)
                if i >= 2 * NH - 2:
                    last.then_inc(s("simw_ps"), 1)

            pe.wait_ge(s("ffn_in"), 64)
            pe.wait_ge(s("xn1_t_ready"), B)
            for g in range(B * P // GROUP):
                cols = slice(g * GROUP, (g + 1) * GROUP)
                for c in range(NC):
                    n = g * NC + c
                    reuse(pe, "h_t_ready", n - 1)
                    for d in range(G):
                        last = mm(bank[c % 2], wup_sb[:, d, c * P:(c + 1) * P], xn1_t[:, d, cols], start=d == 0, stop=d == G - 1)
                    last.then_inc(s("up_ps"), 1)
                reuse(pe, "hp_t_ready", g)
                for c in range(NC):
                    pe.wait_ge(s("h_t_ready"), g * NC + c + 1)
                    last = mm(bank[2], wdown_sb[:, c, :], h_t[:, c, :], start=c == 0, stop=c == NC - 1)
                last.then_inc(s("down_ps"), 1)
            pe.wait_ge(s("hp_t_ready"), B * P // GROUP)
            pe.wait_ge(s("simw_ready"), 4)

            def similarities(t):
                pe.wait_ge(s("hp_ready"), t + 1)
                reuse(pe, "top_ready", t)
                for side in range(2):
                    last = mm(bank[side][:, 0:NH * NK], hp[:, :], simw[:, side * NH * NK:(side + 1) * NH * NK], start=True, stop=True)
                last.then_inc(s("sim_ps"), 1)

            def inner(t):
                for q in range(4):
                    reuse(pe, "z_rest_ready", 4 * t + (q - 1))
                    for c in range(4):
                        last = mm(bank[3 + q % 2][:, c * P:(c + 1) * P], down_sb[:, 4 * q + c, :], hp[:, :], start=True, stop=True)
                    last.then_inc(s("z_ps"), 1)

            def turn_by_token(t):
                pe.wait_ge(s("by_token_ready"), t + 1)
                reuse(pe, "by_k_ready", 4 * t)
                for i in range(3):
                    last = transpose(bank[2][:, i * P:(i + 1) * P], by_token[:, i, :, :].rearrange("p s k -> p (s k)"))
                last.then_inc(s("by_k_ps"), 1)

            def gather(t):
                pe.wait_ge(s("pick_r_ready"), t + 1)
                pe.wait_ge(s("z_low_ready"), 4 * (t + 1))
                reuse(pe, "wt_e_ready", 8 * t)
                for q in range(4):
                    if q >= 2:
                        pe.wait_ge(s("z_sel_read"), 4 * t + (q - 1))
                    for j in range(QP):
                        pair = q * QP + j
                        for part in range(3):
                            last = mm(bank[5 + q % 2][:, j * 2 * EC:(j + 1) * 2 * EC].rearrange("p (s c) -> p s c", c=EC), pick_r[:, pair, :],
                                      z_part[:, part, :, :].rearrange("p (s j) c -> p s j c", s=2)[:, :, pair, :], start=part == 0, stop=part == 2)
                    last.then_inc(s("z_sel_ps"), 1)

            def scatter(t):
                pe.wait_ge(s("wt_hi_ready"), t + 1)
                pe.wait_ge(s("z_sel_read"), 4 * (t + 1))
                for q in range(4):
                    if q >= 2:
                        pe.wait_ge(s("wt_e_ready"), 8 * t + (2 * q - 2))
                    for j in range(QP):
                        pair = q * QP + j
                        for part in range(3):
                            last = mm(bank[5 + q % 2][:, j * 2 * EC:(j + 1) * 2 * EC], pick_k[:, :, pair], wt_hi[:, part, :, pair],
                                      start=part == 0, stop=part == 2)
                    last.then_inc(s("wt_e_ps"), 1)

            def combine(t):
                pe.wait_ge(s("wt_e_ready"), 8 * (t + 1))
                reuse(pe, "y_ready", t)
                for c in range(EC):
                    last = mm(bank[7][:, 0:D], wt_e[:, c, :], up_sb[:, c, :], start=c == 0, stop=c == EC - 1)
                last.then_inc(s("out_ps"), 1)

            def experts(t):
                gather(t)
                similarities(t + 1)
                inner(t + 1)
                scatter(t)
                combine(t)
                turn_by_token(t + 1)

            similarities(0)
            inner(0)
            turn_by_token(0)
            tiles(pe, experts)
            gather(B - 1)
            scatter(B - 1)
            combine(B - 1)


def kernel(**inputs):
    import numpy as np
    import concourse.bacc as bacc
    from concourse import mybir as _mybir
    from concourse.bass_utils import run_bass_kernel_spmd

    a = {k.removeprefix("L0_"): np.asarray(v) for k, v in inputs.items()}
    D, H, HD, P, DCA = 256, 16, 16, 128, 16

    def heads_apart(w):
        return w.reshape(*w.shape[:-1], H, 2, HD).swapaxes(-3, -2).reshape(*w.shape[:-1], 2 * D)

    xn = [a["xattn_qn_w"], a["xattn_qn_b"], a["xattn_kn_w"], a["xattn_kn_b"], a["xattn_kn_dca_w"], a["xattn_kn_dca_b"]]
    keys = a["ffn_keys"].transpose(2, 0, 3, 1)
    keys = keys.reshape(8, P, keys.shape[3]).transpose(1, 0, 2)
    laid = {
        "x": a["x"],
        "y_t": a["ctx_1024"].swapaxes(1, 2),
        "gates": np.concatenate([a["g_xattn"], a["g_ffn"]]),
        "w_q": a["xattn_Wq"],
        "b_q": a["xattn_bq"],
        "w_kv": np.stack([heads_apart(np.concatenate([a["xattn_Wk"], a["xattn_Wv"]], 1)), a["xattn_Wkv_dca"]]),
        "b_kv": np.stack([heads_apart(np.concatenate([a["xattn_bk"], a["xattn_bv"]])), a["xattn_bkv_dca"]]),
        "ln_wb": np.stack([np.tile(v, P // HD) for v in xn], 1),
        "w_o": a["xattn_Wo"],
        "b_o": a["xattn_bo"],
        "w_up_t": a["ffn_W_up"].T,
        "b_up": a["ffn_b_up"].reshape(-1, P).T,
        "w_down_t": a["ffn_W_down"].T,
        "b_down": a["ffn_b_down"].reshape(P, 1),
        "w_ret": a["ffn_W_q"],
        "keys_t": keys,
        "down_t": a["ffn_down_embed"].T,
        "up": a["ffn_up_embed"],
    }
    nc = bacc.Bacc("TRN2", target_bir_lowering=False, num_devices=1)
    arrays, args = {}, []
    for name, v in laid.items():
        v = np.ascontiguousarray(v)
        arrays[name] = v
        args.append(nc.dram_tensor(name, v.shape, _mybir.dt.from_np(v.dtype), kind="ExternalInput").ap())
    scratch = nc.dram_tensor("lo_scratch", (8, 64, 2, 64), _mybir.dt.bfloat16, kind="Internal").ap()
    out = nc.dram_tensor("out", (8, P, D), _mybir.dt.float32, kind="ExternalOutput").ap()
    gated_xattn_peer_kernel(nc, *args, scratch, out)
    r = run_bass_kernel_spmd(nc, [arrays], core_ids=[0])
    return r.results[0]["out"]
```

```python
from contextlib import ExitStack

import concourse.bass as bass
from concourse import mybir


def gated_xattn_peer_kernel(
    nc: bass.Bass,
    x: bass.AP,
    x_t: bass.AP,
    y_t: bass.AP,
    gates: bass.AP,
    w_q: bass.AP,
    b_q: bass.AP,
    w_kv: bass.AP,
    b_kv: bass.AP,
    ln_wb: bass.AP,
    w_o: bass.AP,
    b_o: bass.AP,
    w_up_t: bass.AP,
    b_up: bass.AP,
    w_down_t: bass.AP,
    b_down: bass.AP,
    w_ret: bass.AP,
    keys_t: bass.AP,
    down_t: bass.AP,
    up: bass.AP,
    lo_scratch: bass.AP,
    out: bass.AP,
):
    f32 = mybir.dt.float32
    bf16 = mybir.dt.bfloat16
    u32 = mybir.dt.uint32
    i32 = mybir.dt.int32
    ALU = mybir.AluOpType
    ACT = mybir.ActivationFunctionType
    X = mybir.AxisListType.X

    P = 128
    B, S, D = x.shape
    DY, KEYS = y_t.shape[1:]
    DCA = 16
    MAIN = KEYS - DCA
    H, HD = 16, D // 16
    G = D // P
    HG = H // G
    DC = w_up_t.shape[1]
    NC = DC // P
    NK = keys_t.shape[2]
    NH, K = 8, 8
    HK = NH * K
    NE = 2048
    EC = NE // P
    PAIRS = P // 2
    QP = 16
    EPS_X, EPS_QK = 1e-5, 1e-6
    SCALE = HD ** -0.5

    ctx = ExitStack()
    with ctx:
        def sb(name, shape, dt=f32):
            return ctx.enter_context(nc.sbuf_tensor(name, shape, dt))

        def ps(name, shape, dt=f32):
            return ctx.enter_context(nc.psum_tensor(name, shape, dt))

        def sem(name):
            return ctx.enter_context(nc.semaphore(name))

        ident = sb("ident", [P, P])
        minus_ident = sb("minus_ident", [P, P], bf16)
        head_mask = sb("head_mask", [P, HG])
        side_mask = sb("side_mask", [P, 2])
        mean_w = sb("mean_w", [P, P])
        iota_p = sb("iota_p", [P, 1])
        iota8 = sb("iota8", [P, K, 2 * HK], bf16)
        iota_hi = sb("iota_hi", [P, 2 * EC, PAIRS], bf16)
        iota_lo = sb("iota_lo", [P, P, PAIRS], bf16)
        minus_half = sb("minus_half", [P, B])
        bqkv = sb("bqkv", [P, 3 * D])
        wb = sb("wb", [P, 6])
        bo_t = sb("bo_t", [P, D])
        gate_in = sb("gate_in", [P, 2])
        gate = sb("gate", [P, 2])
        half_gate = sb("half_gate", [P, 1])
        wup_sb = sb("wup_sb", [P, G, DC])
        bup_sb = sb("bup_sb", [P, NC])
        wdown_sb = sb("wdown_sb", [P, NC, P])
        bdown_sb = sb("bdown_sb", [P, 1])
        keys_sb = sb("keys_sb", [P, 8, NK])
        simw = sb("simw", [P, 2 * NH * NK])
        down_sb = sb("down_sb", [P, EC, P])
        up_sb = sb("up_sb", [P, EC, D])
        means = sb("means", [P, 6, H])

        area = sb("area", [P, 4 * H * P + B * H * 2 * (HD + 1) + 4 * D])
        area2 = sb("area2", [P, 4096])
        area4 = sb("area4", [P, EC * P])
        area5 = sb("area5", [P, 4 * D + 3 * P])

        def heads_area(i, h):
            return area[:, i * H * P:(i + 1) * H * P].rearrange("p (h c) -> p h c", h=h)

        def mask_area(i, a):
            return area[:, i * PAIRS * P // 2:(i + 1) * PAIRS * P // 2].bitcast(bf16).rearrange("p (a b) -> p a b", a=a)

        k_diag = heads_area(0, H).rearrange("p (g h) c -> p g h c", g=G)
        shifted = heads_area(1, H)
        prob = heads_area(2, H)
        prob_t = heads_area(3, H)
        SUM = HD
        o = 4 * H * P
        v_ext = area[:, o:o + B * H * 2 * (HD + 1)].rearrange("p (b h s d) -> p b h s d", b=B, h=H, s=2)
        o += B * H * 2 * (HD + 1)
        bv_side = area[:, o:o + 2 * D].rearrange("p (s n) -> p s n", s=2)
        o += 2 * D
        ctx_part = area[:, o:o + 2 * D].rearrange("p (h s d) -> p h s d", h=H, s=2)
        wq_sb = area2[:, 0:512].rearrange("p (g n) -> p g n", g=G)
        wkv_sb = area2[:, 512:1536].rearrange("p (a n) -> p a n", a=2)
        wo_sb = area2[:, 1536:2048].rearrange("p (g n) -> p g n", g=G)
        qk = area2[:, 2048:2560].rearrange("p (h d) -> p h d", d=HD)
        qk_sq = area2[:, 2560:3072].rearrange("p (h d) -> p h d", d=HD)
        qkn = area2[:, 3072:3584].rearrange("p (h d) -> p h d", d=HD)
        q_t = area2[:, 3584:3840].rearrange("p (g c) -> p g c", g=G)
        k_t = area2[:, 3840:4096].rearrange("p (g c) -> p g c", g=G)
        wret_sb = area4[:, 0:1024].rearrange("p (c n) -> p c n", n=P)
        x1 = sb("x1", [P, B, D])
        xstat = sb("xstat", [P, B, 6])
        xmv = sb("xmv", [P, B, 2])
        xvar = sb("xvar", [P, B])
        xrstd = sb("xrstd", [P, B])
        x_tile = area5[:, 0:D].rearrange("p (g c) -> p g c", g=G)
        ctx_sb = area5[:, D:2 * D]
        ctx_t = area5[:, 2 * D:3 * D].rearrange("p (g c) -> p g c", g=G)
        xn1 = area5[:, 3 * D:4 * D]
        y_main = area5[:, 4 * D:4 * D + P]
        y_dca = area5[:, 4 * D + P:4 * D + 2 * P]
        qk_ss = sb("qk_ss", [P, 2 * H])
        qk_var = sb("qk_var", [P, 2 * H])
        qk_bits = sb("qk_bits", [P, 2 * H], i32)
        root = sb("root", [P, 2 * H])
        root_sq = sb("root_sq", [P, 2 * H])
        root_err = sb("root_err", [P, 2 * H])
        smax = sb("smax", [P, 2, H])
        rsum = sb("rsum", [P, H, 2])
        stat1 = sb("stat1", [P, 6])
        mv1 = sb("mv1", [P, 2])
        var1 = sb("var1", [P, 1])
        rstd1 = sb("rstd1", [P, 1])
        xn1_t = sb("xn1_t", [P, G, B * P])

        h_t = sb("h_t", [P, NC, P])
        hp_t = sb("hp_t", [P, B * P])
        hp = sb("hp", [P, P])
        top_v = sb("top_v", [P, 2 * NH, K])
        top_i = sb("top_i", [P, 2 * NH, K], u32)
        top_f = sb("top_f", [P, K, 2 * NH], bf16)
        sums = area5[:, 0:NH * K * K].rearrange("p (h a b) -> p h a b", a=K, b=K)
        best = sb("best", [P, NH, K])
        pick = sb("pick", [P, NH, K], u32)
        pick2 = sb("pick2", [P, 2, HK], u32)
        pick2f = sb("pick2f", [P, 2 * HK], bf16)
        one_hot = area5[:, 512:1024].bitcast(bf16).rearrange("p (a k) -> p a k", a=K)
        chosen = sb("chosen", [P, K, 2 * HK], bf16)
        side_i = sb("side_i", [P, K, 2, NH])
        expert_u = sb("expert_u", [P, HK], u32)
        part_u = sb("part_u", [P, 2, HK], u32)
        lo_bf = sb("lo_bf", [P, HK], bf16)
        by_token = area5[:, 1024:1408].rearrange("p (i s k) -> p i s k", i=3, s=2)
        bshift = sb("bshift", [P, NH, K])
        bexp = sb("bexp", [P, NH, K])
        bsum = sb("bsum", [P, NH])
        brec = sb("brec", [P, NH])
        lo_hi_k = sb("lo_hi_k", [P, 2, PAIRS], bf16)
        prob_k = sb("prob_k", [P, PAIRS])
        lo_all = mask_area(0, PAIRS)
        pick_r = mask_area(1, PAIRS)
        pick_k = mask_area(2, P)
        pick_hi = sb("pick_hi", [P, 2 * EC, PAIRS], bf16)
        z_part = area2[:, 0:3072].bitcast(bf16).rearrange("p (i t c) -> p i t c", i=3, c=EC)
        z_sel = area2[:, 3072:4096].rearrange("p (j c) -> p j c", c=EC)
        wt_e = area4[:, :].rearrange("p (c t) -> p c t", t=P)
        z_k = sb("z_k", [P, PAIRS])
        act_in = sb("act_in", [P, PAIRS])
        act_tanh = sb("act_tanh", [P, PAIRS])
        wt = sb("wt", [P, PAIRS])
        wt_rest = sb("wt_rest", [P, PAIRS])
        wt_part = sb("wt_part", [P, 3, PAIRS], bf16)
        wt_hi = sb("wt_hi", [P, 3, 2 * EC, PAIRS], bf16)
        y_out = sb("y_out", [P, D])

        bank = [ps(f"bank{i}", [P, 512]) for i in range(4)]
        wide = ps("wide", [P, 2048])
        bank += [wide[:, i * 512:(i + 1) * 512] for i in range(4)]
        bank = [b[:, :] for b in bank]

        made = {}

        def s(name):
            if name not in made:
                made[name] = ctx.enter_context(nc.semaphore(name))
            return made[name]

        def reuse(eng, name, count):
            if not isinstance(count, int) or count > 0:
                eng.wait_ge(s(name), count)

        def wait_apart(eng, name):
            eng.sem_inc(s(name), 1)

        class Chain:
            def __init__(self, eng, name):
                self.eng, self.sem, self.base, self.n = eng, s(name), 0, 0

            def link(self, ins, meanwhile=None):
                self.n += 1
                ins.then_inc(self.sem, 1)
                if meanwhile:
                    meanwhile()
                self.eng.wait_ge(self.sem, self.base + self.n)

        def steps(eng, body, ahead, chain=None, behind=0, first=None, before={}):
            def step(t):
                if t in before:
                    before[t]()
                n0 = chain.n if chain else 0
                body(t)
                return chain.n - n0 if chain else 0

            for t in range(-ahead if first is None else first, 1 + behind):
                count = step(t)
            done = chain.base + chain.n if chain else 0
            with eng.Fori(1 + behind, B - ahead) as t:
                if chain:
                    chain.base, chain.n = t * count + (done - (1 + behind) * count), 0
                body(t)
                assert not chain or chain.n == count
            if chain:
                chain.base, chain.n = done + (B - ahead - 1 - behind) * count, 0
            for t in range(B - ahead, B + behind):
                step(t)

        def at(t, *which):
            return isinstance(t, int) and t in which

        def there(t):
            return not isinstance(t, int) or 0 <= t < B

        sides = ((0, 0, MAIN), (1, MAIN, KEYS))
        z_bank = (5, 6, 3, 4)
        pair_bank = (5, 6, 7, 5)
        block = ctx.enter_context(nc.Block())

        @block.sync
        def _(sp):
            def load_tile(t):
                reuse(sp, "v_ps", t)
                sp.dma_start(x_tile[:, :, :], x_t[bass.ds(t, 1)].rearrange("a p g n -> (a p) g n")).then_inc(s("tile_in"), 16)
                sp.dma_start(y_main[:, 0:MAIN], y_t[bass.ds(t, 1), :, 0:MAIN].rearrange("a p n -> (a p) n")).then_inc(s("tile_in"), 16)
                sp.dma_start(y_dca[:, MAIN:P], y_t[bass.ds(t, 1), :, MAIN:P].rearrange("a p n -> (a p) n")).then_inc(s("tile_in"), 16)

            sp.dma_start(wq_sb[:, :, :], w_q.rearrange("(g p) n -> p g n", p=P)).then_inc(s("wqkv_in"), 16)
            sp.dma_start(wkv_sb[:, :, :], w_kv.rearrange("a p n -> p a n")).then_inc(s("wqkv_in"), 16)
            sp.dma_start(bqkv[:, 0:D], b_q.unsqueeze(0).broadcast_to([P, D])).then_inc(s("wqkv_in"), 16)
            sp.dma_start(bqkv[0:MAIN, D:3 * D], b_kv[0:1, :].broadcast_to([MAIN, 2 * D])).then_inc(s("wqkv_in"), 16)
            sp.dma_start(bqkv[MAIN:P, D:3 * D], b_kv[1:2, :].broadcast_to([DCA, 2 * D])).then_inc(s("wqkv_in"), 16)
            sp.dma_start(x1[:, :, :], x.rearrange("b p n -> p b n")).then_inc(s("x_in"), 16)
            sp.wait_ge(s("y_zero"), 2)
            load_tile(0)
            sp.dma_start(gate_in[:, :], gates.unsqueeze(0).broadcast_to([P, 2])).then_inc(s("gate_in"), 16)
            sp.dma_start(bo_t[:, :], b_o.unsqueeze(0).broadcast_to([P, D])).then_inc(s("gate_in"), 16)
            sp.dma_start(wb[:, :], ln_wb).then_inc(s("wb_in"), 16)
            sp.dma_start(wret_sb[:, :, :], w_ret.rearrange("(c p) n -> p c n", p=P)).then_inc(s("ret_in"), 16)
            sp.dma_start(keys_sb[:, :, :], keys_t).then_inc(s("ret_in"), 16)
            load_tile(1)
            sp.dma_start(wo_sb[:, :, :], w_o.rearrange("(g p) n -> p g n", p=P)).then_inc(s("wo_in"), 16)
            load_tile(2)
            sp.dma_start(wup_sb[:, :, :], w_up_t.rearrange("(g p) n -> p g n", p=P)).then_inc(s("ffn_in"), 16)
            sp.dma_start(bup_sb[:, :], b_up).then_inc(s("ffn_in"), 16)
            sp.dma_start(wdown_sb[:, :, :], w_down_t.rearrange("(c p) n -> p c n", p=P)).then_inc(s("ffn_in"), 16)
            sp.dma_start(bdown_sb[:, :], b_down).then_inc(s("ffn_in"), 16)
            load_tile(3)
            sp.dma_start(down_sb[:, :, :], down_t.rearrange("p (c r) -> p c r", r=P)).then_inc(s("experts_in"), 16)
            load_tile(4)
            sp.dma_start(up_sb[:, :, :], up.rearrange("(c r) n -> r c n", r=P)).then_inc(s("experts_in"), 16)
            with sp.Fori(5, B) as t:
                load_tile(t)

            def spread_lo(t):
                row = lo_scratch[bass.ds(t, 1)]
                sp.wait_ge(s("lo_ready"), t + 1)
                for side in range(2):
                    sp.dma_start(row[:, :, side, :].rearrange("a j k -> (a j) k"),
                                 lo_bf[side * PAIRS:(side + 1) * PAIRS, :]).then_inc(s("lo_stored"), 16)
                sp.wait_ge(s("lo_stored"), (t + 1) * 32)
                reuse(sp, "pick_r_ready", t)
                sp.dma_start(lo_all[:, :, :].rearrange("p a b -> p (a b)"),
                             row.rearrange("a j s k -> a (j s k)").broadcast_to([P, PAIRS * P])).then_inc(s("lo_all_in"), 16)

            def store(t):
                sp.wait_ge(s("y_ready"), t + 1)
                sp.dma_start(out[bass.ds(t, 1)].rearrange("a p n -> (a p) n"), y_out[:, :]).then_inc(s("y_stored"), 16)

            def experts(t):
                if there(t + 2):
                    spread_lo(t + 2)
                if there(t):
                    store(t)

            steps(sp, experts, 2)
            sp.wait_ge(s("y_stored"), 16 * B)

        @block.gpsimd
        def _(pool):
            chain = Chain(pool, "pool_step")
            link = chain.link
            pool.memset(y_main[:, :], 0.0).then_inc(s("y_zero"), 1)
            pool.memset(y_dca[:, :], 0.0).then_inc(s("y_zero"), 1)
            link(pool.memset(minus_half[:, :], -0.5))
            link(pool.memset(ident[:, :], 0.0))
            pool.affine_select(out=ident[:, :], in_=ident[:, :], compare_op=ALU.not_equal, fill=1.0, base=0,
                               pattern=[[-1, P]], channel_multiplier=1).then_inc(s("ident_ready"), 1)
            link(pool.memset(head_mask[:, :], 1.0))
            link(pool.affine_select(out=head_mask[:, :], in_=head_mask[:, :], compare_op=ALU.is_ge, fill=0.0,
                                    base=0, pattern=[[-HD, HG]], channel_multiplier=1))
            link(pool.affine_select(out=head_mask[:, :], in_=head_mask[:, :], compare_op=ALU.is_ge, fill=0.0,
                                    base=HD - 1, pattern=[[HD, HG]], channel_multiplier=-1))
            link(pool.memset(side_mask[:, :], 1.0))
            link(pool.affine_select(out=side_mask[:, 0:1], in_=side_mask[:, 0:1], compare_op=ALU.is_ge, fill=0.0,
                                    base=MAIN - 1, pattern=[[0, 1]], channel_multiplier=-1))
            pool.affine_select(out=side_mask[:, 1:2], in_=side_mask[:, 1:2], compare_op=ALU.is_ge, fill=0.0,
                               base=-MAIN, pattern=[[0, 1]], channel_multiplier=1).then_inc(s("side_mask_ready"), 1)
            pool.memset(mean_w[:, :], 1.0 / D).then_inc(s("mean_w_ready"), 1)
            pool.wait_ge(s("xvar_ready"), 1)
            pool.tensor_tensor(xrstd[:, :], xvar[:, :], minus_half[:, 0:B], ALU.pow).then_inc(s("xrstd_ready"), 1)

            pool.wait_ge(s("bo_ready"), 1)
            pool.tensor_tensor(x1[:, :, :], x1[:, :, :], bo_t[:, :].unsqueeze(1).broadcast_to([P, B, D]), ALU.add).then_inc(s("x1_ready"), 1)

            pool.iota(iota_p[:, :], pattern=[[0, 1]], base=0, channel_multiplier=1, allow_small_or_imprecise_dtypes=True)
            pool.iota(iota8[:, :, :], pattern=[[1, K], [0, 2 * HK]], base=0, channel_multiplier=0, allow_small_or_imprecise_dtypes=True)
            pool.iota(iota_hi[:, :, :], pattern=[[1, 2 * EC], [0, PAIRS]], base=0, channel_multiplier=0, allow_small_or_imprecise_dtypes=True)

            def diagonals(t):
                pool.wait_ge(s("k_t_ready"), 2 * (t + 1))
                for g in range(G):
                    reuse(pool, "scores_ready", G * t + (g + 1 - G))
                    pool.tensor_tensor(k_diag[:, g, :, :], k_t[:, g, :].unsqueeze(1).broadcast_to([P, HG, P]),
                                       head_mask[:, :].unsqueeze(2).broadcast_to([P, HG, P]), ALU.mult).then_inc(s("k_diag_ready"), 1)

            def rstd_x1(t):
                pool.wait_ge(s("var1_ready"), t + 1)
                reuse(pool, "xn1_ready", t)
                pool.tensor_tensor(rstd1[:, :], var1[:, :], minus_half[:, 0:1], ALU.pow).then_inc(s("rstd1_ready"), 1)

            def attention(t):
                if there(t - 1):
                    rstd_x1(t - 1)
                if there(t + 1):
                    diagonals(t + 1)

            steps(pool, attention, 2, behind=1)
            pool.iota(iota_lo[:, :, :], pattern=[[1, P], [0, PAIRS]], base=0, channel_multiplier=0,
                      allow_small_or_imprecise_dtypes=True).then_inc(s("iota_ready"), 1)

        @block.scalar
        def _(act):
            act.wait_ge(s("gate_in"), 32)
            act.activation(gate[:, :], gate_in[:, :], ACT.Tanh).then_inc(s("gate_ready"), 1)
            act.wait_ge(s("wb_in"), 16)

            def squares(t):
                act.wait_ge(s("qk_ready"), t + 1)
                reuse(act, "qk_ss_ready", t)
                act.activation(qk_sq[:, :, :], qk[:, :, :], ACT.Square).then_inc(s("qk_sq_ready"), 1)

            def take_qk(t):
                tq = bank[3][:, 0:D].rearrange("p (g c) -> p g c", c=P)
                tk = bank[3][:, D:2 * D].rearrange("p (g c) -> p g c", c=P)
                act.wait_ge(s("qk_t_ps"), t + 1)
                reuse(act, "scores_ready", G * t)
                act.activation(q_t[:, :, :], tq, ACT.Identity, scale=wb[:, 0:1], bias=wb[:, 1:2]).then_inc(s("q_t_ready"), 1)
                reuse(act, "k_diag_ready", G * t)
                act.activation(k_t[:, :, 0:MAIN], tk[:, :, 0:MAIN], ACT.Identity, scale=wb[:, 2:3], bias=wb[:, 3:4]).then_inc(s("k_t_ready"), 1)
                act.activation(k_t[:, :, MAIN:P], tk[:, :, MAIN:P], ACT.Identity, scale=wb[:, 4:5], bias=wb[:, 5:6]).then_inc(s("k_t_ready"), 1)

            def exps(t):
                for g in range(G):
                    hs = slice(g * HG, (g + 1) * HG)
                    act.wait_ge(s("shifted_ready"), G * t + g + 1)
                    reuse(act, "prob_t_ps", G * t + (g + 1 - G))
                    act.activation(prob[:, hs, :], shifted[:, hs, :], ACT.Exp, scale=SCALE).then_inc(s("prob_ready"), 1)

            def take_prob(t):
                for g in range(G):
                    hs = slice(g * HG, (g + 1) * HG)
                    act.wait_ge(s("prob_t_ps"), G * t + g + 1)
                    reuse(act, "pv_ps", G * t + (g + 1 - G))
                    act.activation(prob_t[:, hs, :].rearrange("p h c -> p (h c)"), wide[:, g * HG * P:(g + 1) * HG * P],
                                   ACT.Copy).then_inc(s("prob_t_ready"), 1)

            def take_ctx(t):
                act.wait_ge(s("ctx_t_ps"), t + 1)
                reuse(act, "attn_ps", t)
                act.activation(ctx_t[:, :, :].rearrange("p g c -> p (g c)"), bank[3][:, 0:D], ACT.Copy).then_inc(s("ctx_t_ready"), 1)

            def take_xn1(t):
                act.wait_ge(s("xn1_t_ps"), t + 1)
                act.activation(xn1_t[:, :, bass.ds(t * P, P)], bank[3][:, 0:D].rearrange("p (g c) -> p g c", c=P),
                               ACT.Copy).then_inc(s("xn1_t_ready"), 1)

            def attention(t):
                if there(t):
                    exps(t)
                if there(t + 1):
                    take_qk(t + 1)
                if there(t + 2):
                    squares(t + 2)
                if there(t):
                    take_prob(t)
                if there(t - 1):
                    take_xn1(t - 1)
                if there(t):
                    take_ctx(t)

            def take_simw():
                act.wait_ge(s("simw_ps"), 2)
                for side in range(2):
                    for odd in range(2):
                        act.activation(simw[:, side * NH * NK:(side + 1) * NH * NK].rearrange("p (h o k) -> p h o k", o=2, k=NK)[:, :, odd, :],
                                       bank[4 + side + 2 * odd][:, 0:NH // 2 * NK].rearrange("p (h k) -> p h k", k=NK), ACT.Copy).then_inc(s("simw_ready"), 1)

            def silu_up(t, half):
                if half == 0 and at(t, 0):
                    act.wait_ge(s("ffn_in"), 64)
                reuse(act, "down_ps", t)
                act.wait_ge(s("up_ps"), 2 * t + half + 1)
                for c in range(NC // 2):
                    i = half * NC // 2 + c
                    last = act.activation(h_t[:, i, :], bank[3 + half][:, c * P:(c + 1) * P], ACT.Silu, bias=bup_sb[:, i:i + 1])
                last.then_inc(s("h_t_ready"), 1)

            def take_hp(t):
                act.wait_ge(s("down_ps"), t + 1)
                act.activation(hp_t[:, bass.ds(t * P, P)], bank[2][:, 0:P], ACT.Identity, bias=bdown_sb[:, 0:1]).then_inc(s("hp_ready"), 1)
                reuse(act, "sim_ps", t)
                act.activation(hp[:, :], bank[2][:, 0:P], ACT.Identity, bias=bdown_sb[:, 0:1]).then_inc(s("hp_ready"), 1)

            def part_z(t, part, q):
                left = ("z_ps", "z_rest_ps", "z_low_ps")[part]
                if part == q == 0:
                    reuse(act, "z_sel_ps", 4 * t)
                act.wait_ge(s(left), 4 * t + q + 1)
                act.activation(z_part[:, part, :, 4 * q:4 * q + 4].rearrange("p t c -> p c t"),
                               bank[z_bank[q]].rearrange("p (c t) -> p c t", t=P),
                               ACT.Copy).then_inc(s(("z_top_ready", "z_mid_ready", "z_low_ready")[part]), 1)

            def exp_best(t):
                act.wait_ge(s("bshift_ready"), t + 1)
                reuse(act, "by_token_ready", t)
                act.activation(bexp[:, :, :], bshift[:, :, :], ACT.Exp).then_inc(s("bexp_ready"), 1)

            def take_by_k(t):
                act.wait_ge(s("by_k_ps"), t + 1)
                reuse(act, "pick_k_ready", t)
                reuse(act, "act_in_ready", t)
                for side in range(2):
                    rows = slice(side * PAIRS, (side + 1) * PAIRS)
                    src = bank[2].rearrange("p (i t) -> p i t", t=P)[rows, :, side * PAIRS:(side + 1) * PAIRS]
                    act.activation(lo_hi_k[rows, :, :], src[:, 0:2, :], ACT.Copy).then_inc(s("by_k_ready"), 1)
                    act.activation(prob_k[rows, :], src[:, 2, :], ACT.Copy).then_inc(s("by_k_ready"), 1)

            def tanh_act(t):
                act.wait_ge(s("act_in_ready"), t + 1)
                reuse(act, "wt_hi_ready", t)
                act.activation(act_tanh[:, :], act_in[:, :], ACT.Tanh, scale=0.5).then_inc(s("act_tanh_ready"), 1)

            def take_wt(t, q):
                if q == 0:
                    reuse(act, "out_ps", t)
                act.wait_ge(s("wt_e_ps"), 4 * t + q + 1)
                for side in range(2):
                    act.activation(
                        wt_e[:, :, side * PAIRS + q * QP:side * PAIRS + (q + 1) * QP].rearrange("p c j -> p j c"),
                        bank[pair_bank[q]].rearrange("p (j s c) -> p j s c", s=2, c=EC)[:, :, side, :],
                        ACT.Copy).then_inc(s("wt_e_ready"), 1)

            def numbers(t):
                act.wait_ge(s("part_ready"), t + 1)
                reuse(act, "by_k_ps", t)
                act.activation(by_token[:, 0, :, :], part_u[:, 0:1, :].broadcast_to([P, 2, HK]), ACT.Copy)
                act.activation(by_token[:, 1, 0, :], part_u[:, 1, :], ACT.Copy)
                act.activation(by_token[:, 1, 1, :], part_u[:, 1, :], ACT.Copy, bias=float(EC)).then_inc(s("numbers_ready"), 1)

            def experts(t):
                if there(t + 2):
                    silu_up(t + 2, 0)
                if there(t):
                    tanh_act(t)
                if there(t + 2):
                    silu_up(t + 2, 1)
                if there(t + 1):
                    part_z(t + 1, 0, 0)
                    part_z(t + 1, 0, 1)
                if there(t + 2):
                    take_hp(t + 2)
                if at(t, -1):
                    exp_best(0)
                    numbers(0)
                if there(t + 1):
                    for part, q in ((1, 0), (1, 1), (0, 2), (2, 0), (2, 1), (0, 3)):
                        part_z(t + 1, part, q)
                    take_by_k(t + 1)
                if there(t):
                    take_wt(t, 0)
                    take_wt(t, 1)
                if there(t + 1):
                    part_z(t + 1, 1, 2)
                    part_z(t + 1, 1, 3)
                if there(t):
                    take_wt(t, 2)
                    take_wt(t, 3)
                if there(t + 1):
                    part_z(t + 1, 2, 2)
                    part_z(t + 1, 2, 3)
                if there(t + 2) and not at(t, -2):
                    exp_best(t + 2)
                    numbers(t + 2)

            steps(act, attention, 2, behind=1, before={-1: take_simw, B: lambda: experts(-2)})
            steps(act, experts, 2, first=-1)

        @block.vector
        def _(dve):
            chain = Chain(dve, "dve_step")
            link = chain.link

            dve.wait_ge(s("wqkv_in"), 80)
            tensors = [wq_sb[:, 0, :], wq_sb[:, 1, :], wkv_sb[:, 0, 0:D], wkv_sb[:, 1, 0:D], bqkv[:, 0:D], bqkv[:, D:2 * D]]
            tensors = [a.rearrange("p (h d) -> p h d", d=HD) for a in tensors]
            for i, a in enumerate(tensors):
                last = dve.tensor_reduce(means[:, i, :], a, X, ALU.add)
            link(last)
            link(dve.tensor_scalar(means[:, :, :], means[:, :, :], 1.0 / HD, None, ALU.mult))
            for i, a in enumerate(tensors):
                last = dve.tensor_tensor(a, a, means[:, i, :].unsqueeze(2).broadcast_to([P, H, HD]), ALU.subtract)
            last.then_inc(s("wqk_ready"), 1)
            dve.wait_ge(s("x_in"), 16)
            for t in range(B):
                last = dve.bn_stats(xstat[:, t, :], x1[:, t, :])
            link(last)
            for t in range(B):
                last = dve.bn_aggr(xmv[:, t, :], xstat[:, t, :])
            link(last)
            dve.tensor_scalar(xvar[:, :], xmv[:, :, 1], EPS_X, None, ALU.add).then_inc(s("xvar_ready"), 1)
            dve.wait_ge(s("mean_ps"), 1)
            for g in range(G):
                last = dve.tensor_tensor(wq_sb[:, g, :], wq_sb[:, g, :], bank[0][:, 0:D], ALU.subtract)
            last.then_inc(s("wq_ready"), 1)
            dve.wait_ge(s("side_mask_ready"), 1)
            for side in range(2):
                dve.tensor_scalar(bv_side[:, side, :], bqkv[:, 2 * D:3 * D], side_mask[:, side:side + 1], None, ALU.mult)
            link(dve.tensor_copy(v_ext[:, :, :, :, SUM].rearrange("p b h s -> p (b h) s"), side_mask[:, :].unsqueeze(1).broadcast_to([P, B * H, 2])))
            dve.wait_ge(s("gate_ready"), 1)
            dve.wait_ge(s("ident_ready"), 1)
            dve.tensor_scalar(minus_ident[:, :], ident[:, :], -1.0, None, ALU.mult).then_inc(s("minus_ident_ready"), 1)
            dve.tensor_scalar(half_gate[:, :], gate[:, 1:2], 0.5, None, ALU.mult)
            dve.tensor_scalar(bo_t[:, :], bo_t[:, :], gate[:, 0:1], None, ALU.mult).then_inc(s("bo_ready"), 1)

            def bias_qkv(t):
                dve.wait_ge(s("qk_ps"), t + 1)
                reuse(dve, "qkn_ready", t)
                dve.scalar_tensor_tensor(qk[:, 0:H, :].rearrange("p h d -> p (h d)"), bank[1][:, 0:D], xrstd[:, bass.ds(t, 1)], bqkv[:, 0:D],
                                         ALU.mult, ALU.add)
                dve.tensor_tensor(qk[:, H:2 * H, :].rearrange("p h d -> p (h d)"), bank[1][:, D:2 * D], bqkv[:, D:2 * D],
                                  ALU.add).then_inc(s("qk_ready"), 1)
                dve.wait_ge(s("v_ps"), t + 1)
                for side in range(2):
                    last = dve.scalar_tensor_tensor(v_ext[:, bass.ds(t, 1), :, side, 0:HD].rearrange("p b h d -> p (b h) d"),
                                                    bank[2][:, 0:D].rearrange("p (h d) -> p h d", d=HD), side_mask[:, side:side + 1],
                                                    bv_side[:, side, :].rearrange("p (h d) -> p h d", d=HD), ALU.mult, ALU.add)
                last.then_inc(s("v_ready"), 1)

            def var_qk(t):
                dve.wait_ge(s("qk_sq_ready"), t + 1)
                dve.tensor_reduce(qk_ss[:, :], qk_sq[:, :, :], X, ALU.add).then_inc(s("qk_ss_ready"), 1)
                dve.wait_ge(s("qk_ss_ready"), t + 1)
                link(dve.tensor_scalar(qk_var[:, :], qk_ss[:, :], 1.0 / HD, EPS_QK, ALU.mult, ALU.add))
                link(dve.tensor_scalar(qk_bits[:, :], qk_var[:, :].bitcast(i32), 1, None, ALU.arith_shift_right))
                link(dve.tensor_scalar(root[:, :].bitcast(i32), qk_bits[:, :], -1.0, float(0x5F3759DF), ALU.mult, ALU.add))
                for _ in range(3):
                    link(dve.scalar_tensor_tensor(root_sq[:, :], root[:, :], -0.5, root[:, :], ALU.mult, ALU.mult))
                    link(dve.tensor_tensor(root_err[:, :], root_sq[:, :], qk_var[:, :], ALU.mult))
                    link(dve.scalar_tensor_tensor(root[:, :], root_err[:, :], 1.5, root[:, :], ALU.add, ALU.mult))

            def norm_qk(t):
                reuse(dve, "qk_t_ps", t)
                dve.tensor_tensor(qkn[:, :, :], qk[:, :, :], root[:, :].unsqueeze(2).broadcast_to([P, 2 * H, HD]),
                                  ALU.mult).then_inc(s("qkn_ready"), 1)

            def softmax_shift(t):
                for g in range(G):
                    hs = slice(g * HG, (g + 1) * HG)
                    sc = wide[:, g * HG * P:(g + 1) * HG * P].rearrange("p (h k) -> p h k", k=KEYS)
                    dve.wait_ge(s("scores_ready"), G * t + g + 1)
                    for side, c0, c1 in sides:
                        last = dve.tensor_reduce(smax[:, side, hs], sc[:, :, c0:c1], X, ALU.max)
                    link(last)
                    reuse(dve, "prob_ready", G * t + (g + 1 - G))
                    for side, c0, c1 in sides:
                        last = dve.tensor_tensor(shifted[:, hs, c0:c1], sc[:, :, c0:c1],
                                                 smax[:, side, hs].unsqueeze(2).broadcast_to([P, HG, c1 - c0]), ALU.subtract)
                    last.then_inc(s("shifted_ready"), 1)

            def take_context(t):
                pv = [bank[1 + g][:, 0:HG * 2 * (HD + 1)].rearrange("p (h s d) -> p h s d", h=HG, s=2) for g in range(G)]
                for g in range(G):
                    dve.wait_ge(s("pv_ps"), G * t + g + 1)
                    last = dve.reciprocal(rsum[:, g * HG:(g + 1) * HG, :], pv[g][:, :, :, SUM])
                link(last)
                for g in range(G):
                    hs = slice(g * HG, (g + 1) * HG)
                    reuse(dve, "ctx_ready", t)
                    last = dve.tensor_tensor(ctx_part[:, hs, :, :], pv[g][:, :, :, 0:HD],
                                             rsum[:, hs, :].unsqueeze(3).broadcast_to([P, HG, 2, HD]), ALU.mult)
                last.then_inc(s("pv_read"), 1)
                dve.wait_ge(s("pv_read"), t + 1)
                reuse(dve, "ctx_t_ps", t)
                dve.tensor_tensor(ctx_sb[:, :].rearrange("p (h d) -> p h d", d=HD), ctx_part[:, :, 0, :], ctx_part[:, :, 1, :],
                                  ALU.add).then_inc(s("ctx_ready"), 1)

            def residual(t):
                row = x1[:, bass.ds(t, 1), :]
                if at(t, 0):
                    dve.wait_ge(s("x1_ready"), 1)
                dve.wait_ge(s("attn_ps"), t + 1)
                dve.scalar_tensor_tensor(row, bank[0][:, 0:D].unsqueeze(1), gate[:, 0:1], row, ALU.mult, ALU.add).then_inc(s("x1_done"), 1)
                dve.wait_ge(s("x1_done"), t + 1)
                wait_apart(dve, "dve_passed")
                link(dve.bn_stats(stat1[:, :], row.rearrange("p a n -> p (a n)")))
                wait_apart(dve, "dve_passed")
                link(dve.bn_aggr(mv1[:, :], stat1[:, :]))
                reuse(dve, "rstd1_ready", t)
                dve.tensor_scalar(var1[:, :], mv1[:, 1:2], EPS_X, None, ALU.add).then_inc(s("var1_ready"), 1)

            def norm_x1(t):
                dve.wait_ge(s("rstd1_ready"), t + 1)
                reuse(dve, "xn1_t_ps", t)
                dve.tensor_scalar(xn1[:, :].unsqueeze(1), x1[:, bass.ds(t, 1), :], mv1[:, 0:1], rstd1[:, :], ALU.subtract, ALU.mult).then_inc(s("xn1_ready"), 1)

            def attention(t):
                if there(t):
                    softmax_shift(t)
                if there(t - 1):
                    residual(t - 1)
                if there(t + 2):
                    bias_qkv(t + 2)
                if there(t - 1):
                    norm_x1(t - 1)
                if there(t + 2):
                    var_qk(t + 2)
                    norm_qk(t + 2)
                if there(t):
                    take_context(t)

            dve.wait_ge(s("xrstd_ready"), 1)
            steps(dve, attention, 2, chain, behind=1)

            def top_keys(t):
                dve.wait_ge(s("sim_ps"), t + 1)
                wait_apart(dve, "dve_passed")
                sims = [bank[side][:, h * NK:(h + 1) * NK] for side in range(2) for h in range(NH)]
                for i, sim in enumerate(sims):
                    last = dve.max(top_v[:, i, :], sim)
                link(last)
                wait_apart(dve, "dve_passed")
                for i, sim in enumerate(sims):
                    last = dve.max_index(top_i[:, i, :], top_v[:, i, :], sim)
                last.then_inc(s("top_ready"), 1)
                dve.tensor_tensor(sums[:, :, :, :], top_v[:, 0:NH, :].unsqueeze(3).broadcast_to([P, NH, K, K]),
                                  top_v[:, NH:2 * NH, :].unsqueeze(2).broadcast_to([P, NH, K, K]), ALU.add)
                dve.wait_ge(s("top_ready"), t + 1)
                link(dve.tensor_copy(top_f[:, :, :], top_i[:, :, :].rearrange("p g a -> p a g")))
                wait_apart(dve, "dve_passed")

            def top_experts(t):
                for h in range(NH):
                    last = dve.max(best[:, h, :], sums[:, h, :, :].rearrange("p a b -> p (a b)"))
                link(last)
                dve.tensor_tensor(bshift[:, :, :], best[:, :, :], best[:, :, 0:1].broadcast_to([P, NH, K]), ALU.subtract).then_inc(s("bshift_ready"), 1)
                for h in range(NH):
                    last = dve.max_index(pick[:, h, :], best[:, h, :], sums[:, h, :, :].rearrange("p a b -> p (a b)"))
                link(last)
                flat = pick[:, :, :].rearrange("p h k -> p (h k)")
                dve.tensor_scalar(pick2[:, 0, :], flat, 3, None, ALU.logical_shift_right)
                link(dve.tensor_scalar(pick2[:, 1, :], flat, K - 1, None, ALU.bitwise_and))
                link(dve.tensor_copy(pick2f[:, :].rearrange("p (k s h) -> p k s h", s=2, h=NH), pick2[:, :, :].rearrange("p s (h k) -> p k s h", k=K)))
                link(dve.tensor_tensor(one_hot[:, :, :], iota8[:, :, :], pick2f[:, :].unsqueeze(1).broadcast_to([P, K, 2 * HK]), ALU.is_equal))

                def sum_exps():
                    dve.wait_ge(s("bexp_ready"), t + 1)
                    dve.tensor_reduce(bsum[:, :], bexp[:, :, :], X, ALU.add)

                def invert_sums():
                    dve.reciprocal(brec[:, :], bsum[:, :])

                def probabilities():
                    reuse(dve, "by_k_ps", t)
                    for side in range(2):
                        last = dve.tensor_tensor(by_token[:, 2, side, :].rearrange("p (h k) -> p h k", k=K), bexp[:, :, :],
                                                 brec[:, :].unsqueeze(2).broadcast_to([P, NH, K]), ALU.mult)
                    last.then_inc(s("by_token_ready"), 1)

                link(dve.tensor_tensor(chosen[:, :, :].rearrange("p a (k g) -> p a k g", k=K), one_hot[:, :, :].rearrange("p a (k g) -> p a k g", k=K),
                                       top_f[:, :, :].unsqueeze(2).broadcast_to([P, K, K, 2 * NH]), ALU.mult))
                sum_exps()
                link(dve.tensor_reduce(side_i[:, :, :, :].rearrange("p k s h -> p (k s h)"), chosen[:, :, :].rearrange("p a x -> p x a"), X, ALU.add))
                invert_sums()
                link(dve.scalar_tensor_tensor(expert_u[:, :].rearrange("p (h k) -> p k h", k=K), side_i[:, :, 0, :], float(NK), side_i[:, :, 1, :],
                                              ALU.mult, ALU.add))
                reuse(dve, "numbers_ready", t)
                dve.tensor_scalar(part_u[:, 0, :], expert_u[:, :], P - 1, None, ALU.bitwise_and)
                dve.tensor_scalar(part_u[:, 1, :], expert_u[:, :], 7, None, ALU.logical_shift_right).then_inc(s("part_ready"), 1)
                probabilities()
                dve.wait_ge(s("part_ready"), t + 1)
                reuse(dve, "lo_stored", 32 * t)
                dve.tensor_copy(lo_bf[:, :], part_u[:, 0, :]).then_inc(s("lo_ready"), 1)

            def mask_rows(t):
                dve.wait_ge(s("lo_all_in"), 16 * (t + 1))
                reuse(dve, "z_sel_ps", 4 * t)
                dve.tensor_scalar(pick_r[:, :, :], lo_all[:, :, :], iota_p[:, 0:1], None, ALU.is_equal).then_inc(s("pick_r_ready"), 1)

            def mask_hi(t):
                dve.wait_ge(s("by_k_ready"), 4 * (t + 1))
                reuse(dve, "wt_hi_ready", t)
                dve.tensor_tensor(pick_hi[:, :, :], lo_hi_k[:, 1:2, :].broadcast_to([P, 2 * EC, PAIRS]), iota_hi[:, :, :],
                                  ALU.is_equal).then_inc(s("pick_hi_ready"), 1)

            def mask_k(t, quarter):
                rows = slice(quarter * P // 4, (quarter + 1) * P // 4)
                reuse(dve, "wt_e_ps", 4 * t)
                last = dve.tensor_tensor(pick_k[:, rows, :], lo_hi_k[:, 0:1, :].broadcast_to([P, P // 4, PAIRS]), iota_lo[:, rows, :], ALU.is_equal)
                if quarter == 3:
                    last.then_inc(s("pick_k_ready"), 1)

            def select_z(t):
                dve.wait_ge(s("pick_hi_ready"), t + 1)
                for q in range(4):
                    dve.wait_ge(s("z_sel_ps"), 4 * t + q + 1)
                    for side in range(2):
                        rows = slice(side * PAIRS, (side + 1) * PAIRS)
                        last = dve.tensor_tensor(z_sel[rows, q * QP:(q + 1) * QP, :],
                                                 bank[pair_bank[q]].rearrange("p (j s c) -> p j s c", s=2, c=EC)[rows, :, side, :],
                                                 pick_hi[rows, side * EC:(side + 1) * EC, q * QP:(q + 1) * QP].rearrange("p c j -> p j c"), ALU.mult)
                    last.then_inc(s("z_sel_read"), 1)
                dve.wait_ge(s("z_sel_read"), 4 * (t + 1))
                link(dve.tensor_reduce(z_k[:, :], z_sel[:, :, :], X, ALU.add))
                dve.tensor_tensor(act_in[:, :], z_k[:, :], prob_k[:, :], ALU.mult).then_inc(s("act_in_ready"), 1)

            def weights(t, meanwhile):
                meanwhile(0)
                dve.wait_ge(s("act_tanh_ready"), t + 1)
                link(dve.scalar_tensor_tensor(wt[:, :], act_tanh[:, :], 1.0, act_in[:, :], ALU.add, ALU.mult), lambda: meanwhile(1))
                link(dve.tensor_copy(wt_part[:, 0, :], wt[:, :]))
                link(dve.tensor_tensor(wt_rest[:, :], wt[:, :], wt_part[:, 0, :], ALU.subtract), lambda: meanwhile(2))
                link(dve.tensor_copy(wt_part[:, 1, :], wt_rest[:, :]))
                reuse(dve, "wt_e_ps", 4 * t)
                link(dve.tensor_tensor(wt_part[:, 2, :], wt_rest[:, :], wt_part[:, 1, :], ALU.subtract), lambda: meanwhile(3))
                for part in range(3):
                    last = dve.tensor_tensor(wt_hi[:, part, :, :], pick_hi[:, :, :],
                                             wt_part[:, part:part + 1, :].broadcast_to([P, 2 * EC, PAIRS]), ALU.mult)
                last.then_inc(s("wt_hi_ready"), 1)

            def finish(t):
                dve.wait_ge(s("out_ps"), t + 1)
                reuse(dve, "y_stored", 16 * t)
                dve.scalar_tensor_tensor(y_out[:, :].unsqueeze(1), bank[2][:, 0:D].unsqueeze(1), half_gate[:, 0:1], x1[:, bass.ds(t, 1), :],
                                         ALU.mult, ALU.add).then_inc(s("y_ready"), 1)

            def experts(t):
                if there(t):
                    select_z(t)
                    weights(t, lambda i: mask_k(t, i))
                if there(t + 1) and not at(t, -1):
                    mask_rows(t + 1)
                    mask_hi(t + 1)
                if there(t + 2):
                    top_keys(t + 2)
                    top_experts(t + 2)
                if at(t, -1):
                    mask_rows(0)
                    mask_hi(0)
                if at(t, B - 1):
                    finish(t - 1)
                if there(t) and not at(t, B - 2):
                    finish(t)

            dve.wait_ge(s("xn1_t_ps"), B)
            dve.wait_ge(s("iota_ready"), 1)
            steps(dve, experts, 2, chain)

        @block.tensor
        def _(pe):
            mm = pe.matmul

            def transpose(to, what):
                return pe.transpose(to, what, ident[:, :])

            def qkv(t):
                pe.wait_ge(s("tile_in"), 48 * (t + 1))
                reuse(pe, "v_ready", t)
                reuse(pe, "pv_read", t - 2)
                for g in range(G):
                    mm(bank[1][:, 0:D], x_tile[:, g, :], wq_sb[:, g, :], start=g == 0, stop=g == G - 1)
                for i, (to, done) in enumerate(((bank[1][:, D:2 * D], "qk_ps"), (bank[2][:, 0:D], "v_ps"))):
                    cols = slice(i * D, (i + 1) * D)
                    mm(to, y_main[:, :], wkv_sb[:, 0, cols], start=True, stop=False)
                    mm(to, y_dca[:, :], wkv_sb[:, 1, cols], start=False, stop=True).then_inc(s(done), 1)

            def turn_qk(t):
                flat = qkn[:, :, :].rearrange("p h d -> p (h d)")
                pe.wait_ge(s("qkn_ready"), t + 1)
                reuse(pe, "ctx_t_ready", t - 1)
                reuse(pe, "k_t_ready", 2 * t)
                for i in range(2 * G):
                    last = transpose(bank[3][:, i * P:(i + 1) * P], flat[:, i * P:(i + 1) * P])
                last.then_inc(s("qk_t_ps"), 1)

            def scores(t):
                pe.wait_ge(s("q_t_ready"), t + 1)
                if at(t, 0):
                    pe.wait_ge(s("simw_ready"), 4)
                for g in range(G):
                    pe.wait_ge(s("k_diag_ready"), G * t + g + 1)
                    reuse(pe, "prob_t_ready", G * t + (g + 1 - G))
                    for half in range(2):
                        last = mm(bank[4 + 2 * g + half], q_t[:, g, :],
                                  k_diag[:, g, half * HG // 2:(half + 1) * HG // 2, :].rearrange("p h c -> p (h c)"), start=True, stop=True)
                    last.then_inc(s("scores_ready"), 1)

            def turn_prob(t):
                for g in range(G):
                    pe.wait_ge(s("prob_ready"), G * t + g + 1)
                    for h in range(g * HG, (g + 1) * HG):
                        last = transpose(wide[:, h * P:(h + 1) * P], prob[:, h, :])
                    last.then_inc(s("prob_t_ps"), 1)

            def context(t):
                pe.wait_ge(s("v_ready"), min(t + 3, B) if isinstance(t, int) else t + 3)
                for g in range(G):
                    pe.wait_ge(s("prob_t_ready"), G * t + g + 1)
                    for h in range(HG):
                        last = mm(bank[1 + g][:, h * 2 * (HD + 1):(h + 1) * 2 * (HD + 1)], prob_t[:, g * HG + h, :],
                                  v_ext[:, bass.ds(t, 1), g * HG + h, :, :].rearrange("p b s d -> p (b s d)"), start=True, stop=True)
                    last.then_inc(s("pv_ps"), 1)

            def turn_ctx(t):
                pe.wait_ge(s("ctx_ready"), t + 1)
                pe.wait_ge(s("k_t_ready"), 2 * min(t + 2, B) if isinstance(t, int) else 2 * (t + 2))
                reuse(pe, "xn1_t_ready", t)
                for g in range(G):
                    last = transpose(bank[3][:, g * P:(g + 1) * P], ctx_sb[:, g * P:(g + 1) * P])
                last.then_inc(s("ctx_t_ps"), 1)

            def project(t):
                if at(t, 0):
                    pe.wait_ge(s("wo_in"), 16)
                pe.wait_ge(s("ctx_t_ready"), t + 1)
                reuse(pe, "x1_done", t)
                for g in range(G):
                    last = mm(bank[0][:, 0:D], ctx_t[:, g, :], wo_sb[:, g, :], start=g == 0, stop=g == G - 1)
                last.then_inc(s("attn_ps"), 1)

            def turn_xn1(t):
                pe.wait_ge(s("xn1_ready"), t + 1)
                pe.wait_ge(s("k_t_ready"), 2 * min(t + 3, B) if isinstance(t, int) else 2 * (t + 3))
                pe.wait_ge(s("ctx_t_ready"), t + 1)
                for g in range(G):
                    last = transpose(bank[3][:, g * P:(g + 1) * P], xn1[:, g * P:(g + 1) * P])
                last.then_inc(s("xn1_t_ps"), 1)

            def attention(t):
                if there(t + 2):
                    qkv(t + 2)
                if there(t + 1):
                    turn_qk(t + 1)
                if there(t):
                    turn_prob(t)
                if there(t - 1):
                    turn_xn1(t - 1)
                if there(t):
                    context(t)
                if there(t + 1):
                    scores(t + 1)
                if there(t):
                    turn_ctx(t)
                    project(t)

            pe.wait_ge(s("ident_ready"), 1)
            pe.wait_ge(s("wqk_ready"), 1)
            pe.wait_ge(s("mean_w_ready"), 1)
            for g in range(G):
                last = mm(bank[0][:, 0:D], mean_w[:, :], wq_sb[:, g, :], start=g == 0, stop=g == G - 1)
            last.then_inc(s("mean_ps"), 1)

            def fold_keys():
                pe.wait_ge(s("ret_in"), 32)
                for i in range(2 * NH):
                    rows = slice(i % 2 * (P // 2), (i % 2 + 1) * (P // 2))
                    h = i % NH // 2
                    last = mm(bank[4 + i // NH + i % 2 * 2][:, h * NK:(h + 1) * NK], wret_sb[rows, i // 2, :], keys_sb[rows, i // 2, :], start=True, stop=True)
                    if i >= 2 * NH - 2:
                        last.then_inc(s("simw_ps"), 1)

            def layer_up(t):
                if at(t, 0):
                    pe.wait_ge(s("ffn_in"), 64)
                    pe.wait_ge(s("xn1_t_ready"), 1)
                reuse(pe, "z_low_ready", 4 * (t - 1))
                for half in range(2):
                    for c in range(NC // 2):
                        i = half * NC // 2 + c
                        for d in range(G):
                            last = mm(bank[3 + half][:, c * P:(c + 1) * P], wup_sb[:, d, i * P:(i + 1) * P], xn1_t[:, d, bass.ds(t * P, P)],
                                      start=d == 0, stop=d == G - 1)
                    last.then_inc(s("up_ps"), 1)

            def layer_down(t):
                pe.wait_ge(s("h_t_ready"), 2 * (t + 1))
                reuse(pe, "by_k_ready", 4 * (t - 1))
                reuse(pe, "y_ready", t - 2)
                for c in range(NC):
                    last = mm(bank[2][:, 0:P], wdown_sb[:, c, :], h_t[:, c, :], start=c == 0, stop=c == NC - 1)
                last.then_inc(s("down_ps"), 1)

            def similarities(t):
                pe.wait_ge(s("hp_ready"), 2 * (t + 1))
                if at(t, 0):
                    pe.wait_ge(s("x1_done"), B)
                reuse(pe, "top_ready", t)
                for side in range(2):
                    last = mm(bank[side][:, 0:NH * NK], hp[:, :], simw[:, side * NH * NK:(side + 1) * NH * NK], start=True, stop=True)
                last.then_inc(s("sim_ps"), 1)

            def inner(t, q):
                if q == 0:
                    reuse(pe, "z_sel_read", 4 * t)
                if q >= 2 and there(t + 1):
                    pe.wait_ge(s("h_t_ready"), 2 * t + (q + 1))
                elif q >= 2:
                    reuse(pe, "z_low_ready", 4 * t)
                for c in range(4):
                    last = mm(bank[z_bank[q]][:, c * P:(c + 1) * P], down_sb[:, 4 * q + c, :], hp_t[:, bass.ds(t * P, P)],
                              start=c == 0, stop=c == 3, skip_group_check=True)
                last.then_inc(s("z_ps"), 1)

            def take_off(t, part, q):
                pe.wait_ge(s(("z_top_ready", "z_mid_ready")[part]), 4 * t + q + 1)
                mm(bank[z_bank[q]].rearrange("p (c t) -> p c t", t=P), minus_ident[:, :], z_part[:, part, :, 4 * q:4 * q + 4].rearrange("p t c -> p c t"),
                   start=False, stop=True, skip_group_check=True).then_inc(s(("z_rest_ps", "z_low_ps")[part]), 1)

            def turn_by_token(t):
                pe.wait_ge(s("by_token_ready"), t + 1)
                pe.wait_ge(s("numbers_ready"), t + 1)
                if there(t + 1):
                    pe.wait_ge(s("hp_ready"), 2 * (t + 2))
                for i in range(3):
                    last = transpose(bank[2][:, i * P:(i + 1) * P], by_token[:, i, :, :].rearrange("p s k -> p (s k)"))
                last.then_inc(s("by_k_ps"), 1)

            def gather(t):
                pe.wait_ge(s("pick_r_ready"), t + 1)
                pe.wait_ge(s("z_low_ready"), 4 * (t + 1))
                reuse(pe, "wt_e_ready", 8 * t)
                for q in range(4):
                    if q == 3:
                        pe.wait_ge(s("z_sel_read"), 4 * t + 1)
                    for j in range(QP):
                        pair = q * QP + j
                        for part in range(3):
                            last = mm(bank[pair_bank[q]][:, j * 2 * EC:(j + 1) * 2 * EC].rearrange("p (s c) -> p s c", c=EC), pick_r[:, pair, :],
                                      z_part[:, part, :, :].rearrange("p (s j) c -> p s j c", s=2)[:, :, pair, :], start=part == 0, stop=part == 2)
                    last.then_inc(s("z_sel_ps"), 1)

            def scatter(t, q):
                if q == 0:
                    pe.wait_ge(s("wt_hi_ready"), t + 1)
                    pe.wait_ge(s("z_sel_read"), 4 * (t + 1))
                    if there(t + 1):
                        pe.wait_ge(s("z_low_ready"), 4 * t + 6)
                if q == 3:
                    pe.wait_ge(s("wt_e_ready"), 8 * t + 2)
                for j in range(QP):
                    pair = q * QP + j
                    for part in range(3):
                        last = mm(bank[pair_bank[q]][:, j * 2 * EC:(j + 1) * 2 * EC], pick_k[:, :, pair], wt_hi[:, part, :, pair],
                                  start=part == 0, stop=part == 2)
                last.then_inc(s("wt_e_ps"), 1)

            def combine(t):
                pe.wait_ge(s("wt_e_ready"), 8 * (t + 1))
                reuse(pe, "y_ready", t)
                pe.wait_ge(s("by_k_ready"), 4 * min(t + 2, B) if isinstance(t, int) else 4 * (t + 2))
                for c in range(EC):
                    last = mm(bank[2][:, 0:D], wt_e[:, c, :], up_sb[:, c, :], start=c == 0, stop=c == EC - 1)
                last.then_inc(s("out_ps"), 1)

            def experts(t):
                if there(t + 2):
                    layer_up(t + 2)
                if there(t + 1):
                    inner(t + 1, 0)
                    inner(t + 1, 1)
                if there(t + 2):
                    layer_down(t + 2)
                if there(t + 1):
                    take_off(t + 1, 0, 0)
                    take_off(t + 1, 0, 1)
                    inner(t + 1, 2)
                if there(t + 2):
                    similarities(t + 2)
                if there(t + 1):
                    take_off(t + 1, 1, 0)
                    take_off(t + 1, 1, 1)
                    inner(t + 1, 3)
                    turn_by_token(t + 1)
                if there(t):
                    scatter(t, 0)
                    scatter(t, 1)
                if there(t + 1):
                    take_off(t + 1, 0, 2)
                    take_off(t + 1, 0, 3)
                if there(t):
                    scatter(t, 2)
                    scatter(t, 3)
                if there(t + 1):
                    take_off(t + 1, 1, 2)
                    take_off(t + 1, 1, 3)
                if there(t) and there(t + 2):
                    combine(t)
                if there(t + 1):
                    gather(t + 1)
                if there(t) and not there(t + 2):
                    combine(t)

            pe.wait_ge(s("wq_ready"), 1)
            steps(pe, attention, 2, behind=1, before={-1: fold_keys, B: lambda: experts(-2)})
            pe.wait_ge(s("experts_in"), 32)
            pe.wait_ge(s("xn1_t_ready"), B)
            pe.wait_ge(s("minus_ident_ready"), 1)
            steps(pe, experts, 2, first=-1)


def kernel(**inputs):
    import numpy as np
    import concourse.bacc as bacc
    from concourse import mybir as _mybir
    from concourse.bass_utils import run_bass_kernel_spmd

    a = {k.removeprefix("L0_"): np.asarray(v) for k, v in inputs.items()}
    D, H, HD, P, DCA = 256, 16, 16, 128, 16

    def heads_apart(w):
        return w.reshape(*w.shape[:-1], H, 2, HD).swapaxes(-3, -2).reshape(*w.shape[:-1], 2 * D)

    xn = [a["xattn_qn_w"], a["xattn_qn_b"], a["xattn_kn_w"], a["xattn_kn_b"], a["xattn_kn_dca_w"], a["xattn_kn_dca_b"]]
    keys = a["ffn_keys"].transpose(2, 0, 3, 1)
    keys = keys.reshape(8, P, keys.shape[3]).transpose(1, 0, 2)
    laid = {
        "x": a["x"],
        "x_t": a["x"].reshape(8, P, D // P, P).transpose(0, 3, 2, 1),
        "y_t": a["ctx_1024"].swapaxes(1, 2),
        "gates": np.concatenate([a["g_xattn"], a["g_ffn"]]),
        "w_q": a["xattn_Wq"],
        "b_q": a["xattn_bq"],
        "w_kv": np.stack([heads_apart(np.concatenate([a["xattn_Wk"], a["xattn_Wv"]], 1)), a["xattn_Wkv_dca"]]),
        "b_kv": np.stack([heads_apart(np.concatenate([a["xattn_bk"], a["xattn_bv"]])), a["xattn_bkv_dca"]]),
        "ln_wb": np.stack([np.tile(v, P // HD) for v in xn], 1),
        "w_o": a["xattn_Wo"],
        "b_o": a["xattn_bo"],
        "w_up_t": a["ffn_W_up"].T,
        "b_up": a["ffn_b_up"].reshape(-1, P).T,
        "w_down_t": a["ffn_W_down"].T,
        "b_down": a["ffn_b_down"].reshape(P, 1),
        "w_ret": a["ffn_W_q"],
        "keys_t": keys,
        "down_t": a["ffn_down_embed"].T,
        "up": a["ffn_up_embed"],
    }
    nc = bacc.Bacc("TRN2", target_bir_lowering=False, num_devices=1)
    arrays, args = {}, []
    for name, v in laid.items():
        v = np.ascontiguousarray(v)
        arrays[name] = v
        args.append(nc.dram_tensor(name, v.shape, _mybir.dt.from_np(v.dtype), kind="ExternalInput").ap())
    scratch = nc.dram_tensor("lo_scratch", (8, 64, 2, 64), _mybir.dt.bfloat16, kind="Internal").ap()
    out = nc.dram_tensor("out", (8, P, D), _mybir.dt.float32, kind="ExternalOutput").ap()
    gated_xattn_peer_kernel(nc, *args, scratch, out)
    r = run_bass_kernel_spmd(nc, [arrays], core_ids=[0])
    return r.results[0]["out"]
```

```python
from contextlib import ExitStack

import concourse.bass as bass
from concourse import mybir


def gated_xattn_peer_kernel(
    nc: bass.Bass,
    x: bass.AP,
    x_t: bass.AP,
    y_t: bass.AP,
    gates: bass.AP,
    w_q: bass.AP,
    b_q: bass.AP,
    w_kv: bass.AP,
    b_kv: bass.AP,
    ln_wb: bass.AP,
    w_o: bass.AP,
    b_o: bass.AP,
    w_up_t: bass.AP,
    b_up: bass.AP,
    w_down_t: bass.AP,
    b_down: bass.AP,
    w_ret: bass.AP,
    keys_t: bass.AP,
    down_t: bass.AP,
    up: bass.AP,
    lo_scratch: bass.AP,
    out: bass.AP,
):
    f32 = mybir.dt.float32
    bf16 = mybir.dt.bfloat16
    u32 = mybir.dt.uint32
    i32 = mybir.dt.int32
    ALU = mybir.AluOpType
    ACT = mybir.ActivationFunctionType
    X = mybir.AxisListType.X

    P = 128
    B, S, D = x.shape
    DY, KEYS = y_t.shape[1:]
    DCA = 16
    MAIN = KEYS - DCA
    H, HD = 16, D // 16
    G = D // P
    HG = H // G
    DC = w_up_t.shape[1]
    NC = DC // P
    NK = keys_t.shape[2]
    NH, K = 8, 8
    HK = NH * K
    NE = 2048
    EC = NE // P
    PAIRS = P // 2
    QP = 16
    EPS_X, EPS_QK = 1e-5, 1e-6
    SCALE = HD ** -0.5

    ctx = ExitStack()
    with ctx:
        def sb(name, shape, dt=f32):
            return ctx.enter_context(nc.sbuf_tensor(name, shape, dt))

        def ps(name, shape, dt=f32):
            return ctx.enter_context(nc.psum_tensor(name, shape, dt))

        def sem(name):
            return ctx.enter_context(nc.semaphore(name))

        ident = sb("ident", [P, P])
        minus_ident = sb("minus_ident", [P, P], bf16)
        head_mask = sb("head_mask", [P, HG])
        side_mask = sb("side_mask", [P, 2])
        mean_w = sb("mean_w", [P, P])
        iota_p = sb("iota_p", [P, 1])
        iota8 = sb("iota8", [P, K, 2 * HK], bf16)
        iota_hi = sb("iota_hi", [P, 2 * EC, PAIRS], bf16)
        iota_lo = sb("iota_lo", [P, P, PAIRS], bf16)
        minus_half = sb("minus_half", [P, B])
        bqk = sb("bqk", [P, 2 * D])
        bv_sb = sb("bv_sb", [2, D])
        side_rows = sb("side_rows", [2, P])
        wb = sb("wb", [P, 6])
        bo_t = sb("bo_t", [P, D])
        gate_in = sb("gate_in", [P, 2])
        gate = sb("gate", [P, 2])
        half_gate = sb("half_gate", [P, 1])
        wup_sb = sb("wup_sb", [P, G, DC])
        bup_sb = sb("bup_sb", [P, NC])
        wdown_sb = sb("wdown_sb", [P, NC, P])
        bdown_sb = sb("bdown_sb", [P, 1])
        keys_sb = sb("keys_sb", [P, 8, NK])
        simw = sb("simw", [P, 2 * NH * NK])
        down_sb = sb("down_sb", [P, EC, P])
        up_sb = sb("up_sb", [P, EC, D])
        means = sb("means", [P, 6, H])

        area = sb("area", [P, 4 * H * P + B * H * 2 * (HD + 1) + 4 * D])
        area2 = sb("area2", [P, 4096])
        area4 = sb("area4", [P, EC * P])
        area5 = sb("area5", [P, 4 * D + 3 * P])

        def heads_area(i, h):
            return area[:, i * H * P:(i + 1) * H * P].rearrange("p (h c) -> p h c", h=h)

        def mask_area(i, a):
            return area[:, i * PAIRS * P // 2:(i + 1) * PAIRS * P // 2].bitcast(bf16).rearrange("p (a b) -> p a b", a=a)

        k_diag = heads_area(0, H).rearrange("p (g h) c -> p g h c", g=G)
        shifted = heads_area(1, H)
        prob = heads_area(2, H)
        prob_t = heads_area(3, H)
        SUM = HD
        o = 4 * H * P
        v_ext = area[:, o:o + B * H * 2 * (HD + 1)].rearrange("p (b h s d) -> p b h s d", b=B, h=H, s=2)
        o += B * H * 2 * (HD + 1)
        ctx_part = area[:, o:o + 2 * D].rearrange("p (h s d) -> p h s d", h=H, s=2)
        wq_sb = area2[:, 0:512].rearrange("p (g n) -> p g n", g=G)
        wkv_sb = area2[:, 512:1536].rearrange("p (a n) -> p a n", a=2)
        wo_sb = area2[:, 1536:2048].rearrange("p (g n) -> p g n", g=G)
        qk = area2[:, 2048:2560].rearrange("p (h d) -> p h d", d=HD)
        qk_sq = area2[:, 2560:3072].rearrange("p (h d) -> p h d", d=HD)
        qkn = area2[:, 3072:3584].rearrange("p (h d) -> p h d", d=HD)
        q_t = area2[:, 3584:3840].rearrange("p (g c) -> p g c", g=G)
        k_t = area2[:, 3840:4096].rearrange("p (g c) -> p g c", g=G)
        wret_sb = area4[:, 0:1024].rearrange("p (c n) -> p c n", n=P)
        x1 = sb("x1", [P, B, D])
        xstat = sb("xstat", [P, B, 6])
        xmv = sb("xmv", [P, B, 2])
        xvar = sb("xvar", [P, B])
        xrstd = sb("xrstd", [P, B])
        x_tile = area5[:, 0:D].rearrange("p (g c) -> p g c", g=G)
        ctx_sb = area5[:, D:2 * D]
        ctx_t = area5[:, 2 * D:3 * D].rearrange("p (g c) -> p g c", g=G)
        xn1 = sb("xn1", [P, D])
        y_main = area5[:, 4 * D:4 * D + P]
        y_dca = area5[:, 4 * D + P:4 * D + 2 * P]
        qk_ss = sb("qk_ss", [P, 2 * H])
        qk_var = sb("qk_var", [P, 2 * H])
        qk_bits = sb("qk_bits", [P, 2 * H], i32)
        root = sb("root", [P, 2 * H])
        root_sq = sb("root_sq", [P, 2 * H])
        root_err = sb("root_err", [P, 2 * H])
        smax = sb("smax", [P, 2, H])
        rsum = sb("rsum", [P, H, 2])
        stat1 = sb("stat1", [P, 6])
        mv1 = sb("mv1", [P, 2])
        var1 = sb("var1", [P, 1])
        rstd1 = sb("rstd1", [P, 1])
        shift1 = sb("shift1", [P, 1])
        xn1_t = sb("xn1_t", [P, G, B * P])

        h_t = sb("h_t", [P, NC, P])
        hp_t = sb("hp_t", [P, B * P])
        hp = sb("hp", [P, P])
        top_v = sb("top_v", [P, 2 * NH, K])
        top_i = sb("top_i", [P, 2 * NH, K], u32)
        top_f = sb("top_f", [P, K, 2 * NH], bf16)
        sums = area5[:, 0:NH * K * K].rearrange("p (h a b) -> p h a b", a=K, b=K)
        best = sb("best", [P, NH, K])
        pick = sb("pick", [P, NH, K], u32)
        pick2 = sb("pick2", [P, 2, HK], u32)
        pick2f = sb("pick2f", [P, 2 * HK], bf16)
        one_hot = area5[:, 512:1024].bitcast(bf16).rearrange("p (a k) -> p a k", a=K)
        chosen = sb("chosen", [P, K, 2 * HK], bf16)
        side_i = sb("side_i", [P, K, 2, NH])
        expert_u = sb("expert_u", [P, HK], u32)
        part_u = sb("part_u", [P, 2, HK], u32)
        lo_bf = sb("lo_bf", [P, HK], bf16)
        by_token = area5[:, 1024:1408].rearrange("p (i s k) -> p i s k", i=3, s=2)
        bshift = sb("bshift", [P, NH, K])
        bexp = sb("bexp", [P, NH, K])
        bsum = sb("bsum", [P, NH])
        brec = sb("brec", [P, NH])
        lo_hi_k = sb("lo_hi_k", [P, 2, PAIRS], bf16)
        prob_k = sb("prob_k", [P, PAIRS])
        lo_all = mask_area(0, PAIRS)
        pick_r = mask_area(1, PAIRS)
        pick_k = mask_area(2, P)
        pick_hi = sb("pick_hi", [P, 2 * EC, PAIRS], bf16)
        z_part = area2[:, 0:3072].bitcast(bf16).rearrange("p (i t c) -> p i t c", i=3, c=EC)
        z_sel = area2[:, 3072:4096].rearrange("p (j c) -> p j c", c=EC)
        wt_e = area4[:, :].rearrange("p (c t) -> p c t", t=P)
        z_k = sb("z_k", [P, PAIRS])
        act_in = sb("act_in", [P, PAIRS])
        act_tanh = sb("act_tanh", [P, PAIRS])
        wt = sb("wt", [P, PAIRS])
        wt_rest = sb("wt_rest", [P, PAIRS])
        wt_part = sb("wt_part", [P, 3, PAIRS], bf16)
        wt_hi = sb("wt_hi", [P, 3, 2 * EC, PAIRS], bf16)
        y_out = sb("y_out", [P, D])

        bank = [ps(f"bank{i}", [P, 512]) for i in range(4)]
        wide = ps("wide", [P, 2048])
        bank += [wide[:, i * 512:(i + 1) * 512] for i in range(4)]
        bank = [b[:, :] for b in bank]

        made = {}

        def s(name):
            if name not in made:
                made[name] = ctx.enter_context(nc.semaphore(name))
            return made[name]

        def reuse(eng, name, count):
            if not isinstance(count, int) or count > 0:
                eng.wait_ge(s(name), count)

        def wait_apart(eng, name):
            eng.sem_inc(s(name), 1)

        class Chain:
            def __init__(self, eng, name):
                self.eng, self.sem, self.base, self.n = eng, s(name), 0, 0

            def link(self, ins, meanwhile=None):
                self.n += 1
                ins.then_inc(self.sem, 1)
                if meanwhile:
                    meanwhile()
                self.eng.wait_ge(self.sem, self.base + self.n)

        def steps(eng, body, ahead, chain=None, behind=0, first=None, before={}):
            def step(t):
                if t in before:
                    before[t]()
                n0 = chain.n if chain else 0
                body(t)
                return chain.n - n0 if chain else 0

            for t in range(-ahead if first is None else first, 1 + behind):
                count = step(t)
            done = chain.base + chain.n if chain else 0
            with eng.Fori(1 + behind, B - ahead) as t:
                if chain:
                    chain.base, chain.n = t * count + (done - (1 + behind) * count), 0
                body(t)
                assert not chain or chain.n == count
            if chain:
                chain.base, chain.n = done + (B - ahead - 1 - behind) * count, 0
            for t in range(B - ahead, B + behind):
                step(t)

        def at(t, *which):
            return isinstance(t, int) and t in which

        def there(t):
            return not isinstance(t, int) or 0 <= t < B

        sides = ((0, 0, MAIN), (1, MAIN, KEYS))
        z_bank = (5, 6, 3, 4)
        up_bank = lambda t: (1, 2) if at(t, 0) else (3, 4)
        down_bank = lambda t: 0 if at(t, 0) else 2
        sim_bank = lambda t: (7, 4) if at(t, 0) else (0, 1)
        xn1_bank = lambda t: 0 if at(t, B - 1) else 3
        gather_bank = lambda t: (5, 6, 7, 4) if at(t, B - 1) else (5, 6, 7, 5)
        scatter_bank = lambda t: (0, 1, 3, 0) if at(t, B - 2) else (5, 6, 7, 5)
        block = ctx.enter_context(nc.Block())

        @block.sync
        def _(sp):
            def load_tile(t):
                reuse(sp, "v_ps", t)
                sp.dma_start(x_tile[:, :, :], x_t[bass.ds(t, 1)].rearrange("a p g n -> (a p) g n")).then_inc(s("tile_in"), 16)
                sp.dma_start(y_main[:, 0:MAIN], y_t[bass.ds(t, 1), :, 0:MAIN].rearrange("a p n -> (a p) n")).then_inc(s("tile_in"), 16)
                sp.dma_start(y_dca[:, MAIN:P], y_t[bass.ds(t, 1), :, MAIN:P].rearrange("a p n -> (a p) n")).then_inc(s("tile_in"), 16)

            sp.dma_start(wq_sb[:, :, :], w_q.rearrange("(g p) n -> p g n", p=P)).then_inc(s("wqkv_in"), 16)
            sp.dma_start(wkv_sb[:, :, :], w_kv.rearrange("a p n -> p a n")).then_inc(s("wqkv_in"), 16)
            sp.dma_start(bqk[:, 0:D], b_q.unsqueeze(0).broadcast_to([P, D])).then_inc(s("wqkv_in"), 16)
            sp.dma_start(bqk[0:MAIN, D:2 * D], b_kv[0:1, 0:D].broadcast_to([MAIN, D])).then_inc(s("wqkv_in"), 16)
            sp.dma_start(bqk[MAIN:P, D:2 * D], b_kv[1:2, 0:D].broadcast_to([DCA, D])).then_inc(s("wqkv_in"), 16)
            sp.dma_start(bv_sb[:, :], b_kv[:, D:2 * D]).then_inc(s("bv_in"), 16)
            sp.dma_start(x1[:, :, :], x.rearrange("b p n -> p b n")).then_inc(s("x_in"), 16)
            sp.wait_ge(s("y_zero"), 2)
            load_tile(0)
            sp.dma_start(gate_in[:, :], gates.unsqueeze(0).broadcast_to([P, 2])).then_inc(s("gate_in"), 16)
            sp.dma_start(bo_t[:, :], b_o.unsqueeze(0).broadcast_to([P, D])).then_inc(s("gate_in"), 16)
            sp.dma_start(wb[:, :], ln_wb).then_inc(s("wb_in"), 16)
            sp.dma_start(wret_sb[:, :, :], w_ret.rearrange("(c p) n -> p c n", p=P)).then_inc(s("ret_in"), 16)
            sp.dma_start(keys_sb[:, :, :], keys_t).then_inc(s("ret_in"), 16)
            load_tile(1)
            sp.dma_start(wo_sb[:, :, :], w_o.rearrange("(g p) n -> p g n", p=P)).then_inc(s("wo_in"), 16)
            load_tile(2)
            sp.dma_start(wup_sb[:, :, :], w_up_t.rearrange("(g p) n -> p g n", p=P)).then_inc(s("ffn_in"), 16)
            sp.dma_start(bup_sb[:, :], b_up).then_inc(s("ffn_in"), 16)
            sp.dma_start(wdown_sb[:, :, :], w_down_t.rearrange("(c p) n -> p c n", p=P)).then_inc(s("ffn_in"), 16)
            sp.dma_start(bdown_sb[:, :], b_down).then_inc(s("ffn_in"), 16)
            load_tile(3)
            sp.dma_start(down_sb[:, :, :], down_t.rearrange("p (c r) -> p c r", r=P)).then_inc(s("experts_in"), 16)
            load_tile(4)
            sp.dma_start(up_sb[:, :, :], up.rearrange("(c r) n -> r c n", r=P)).then_inc(s("experts_in"), 16)
            with sp.Fori(5, B) as t:
                load_tile(t)

            def spread_lo(t):
                row = lo_scratch[bass.ds(t, 1)]
                sp.wait_ge(s("lo_ready"), t + 1)
                for side in range(2):
                    sp.dma_start(row[:, :, side, :].rearrange("a j k -> (a j) k"),
                                 lo_bf[side * PAIRS:(side + 1) * PAIRS, :]).then_inc(s("lo_stored"), 16)
                sp.wait_ge(s("lo_stored"), (t + 1) * 32)
                reuse(sp, "pick_r_ready", t)
                sp.dma_start(lo_all[:, :, :].rearrange("p a b -> p (a b)"),
                             row.rearrange("a j s k -> a (j s k)").broadcast_to([P, PAIRS * P])).then_inc(s("lo_all_in"), 16)

            def store(t):
                sp.wait_ge(s("y_ready"), t + 1)
                sp.dma_start(out[bass.ds(t, 1)].rearrange("a p n -> (a p) n"), y_out[:, :]).then_inc(s("y_stored"), 16)

            def experts(t):
                if there(t + 2):
                    spread_lo(t + 2)
                if there(t):
                    store(t)

            steps(sp, experts, 2)
            sp.wait_ge(s("y_stored"), 16 * B)

        @block.gpsimd
        def _(pool):
            chain = Chain(pool, "pool_step")
            link = chain.link
            pool.memset(y_main[:, :], 0.0).then_inc(s("y_zero"), 1)
            pool.memset(y_dca[:, :], 0.0).then_inc(s("y_zero"), 1)
            link(pool.memset(minus_half[:, :], -0.5))
            link(pool.memset(ident[:, :], 0.0))
            pool.affine_select(out=ident[:, :], in_=ident[:, :], compare_op=ALU.not_equal, fill=1.0, base=0,
                               pattern=[[-1, P]], channel_multiplier=1).then_inc(s("ident_ready"), 1)
            link(pool.memset(head_mask[:, :], 1.0))
            link(pool.affine_select(out=head_mask[:, :], in_=head_mask[:, :], compare_op=ALU.is_ge, fill=0.0,
                                    base=0, pattern=[[-HD, HG]], channel_multiplier=1))
            link(pool.affine_select(out=head_mask[:, :], in_=head_mask[:, :], compare_op=ALU.is_ge, fill=0.0,
                                    base=HD - 1, pattern=[[HD, HG]], channel_multiplier=-1))
            link(pool.memset(side_mask[:, :], 1.0))
            link(pool.affine_select(out=side_mask[:, 0:1], in_=side_mask[:, 0:1], compare_op=ALU.is_ge, fill=0.0,
                                    base=MAIN - 1, pattern=[[0, 1]], channel_multiplier=-1))
            pool.affine_select(out=side_mask[:, 1:2], in_=side_mask[:, 1:2], compare_op=ALU.is_ge, fill=0.0,
                               base=-MAIN, pattern=[[0, 1]], channel_multiplier=1).then_inc(s("side_mask_ready"), 1)
            pool.memset(mean_w[:, :], 1.0 / D).then_inc(s("mean_w_ready"), 1)
            link(pool.memset(side_rows[:, :], 1.0))
            link(pool.affine_select(out=side_rows[:, :], in_=side_rows[:, :], compare_op=ALU.is_ge, fill=0.0,
                                    base=0, pattern=[[1, P]], channel_multiplier=-MAIN))
            pool.affine_select(out=side_rows[:, :], in_=side_rows[:, :], compare_op=ALU.is_ge, fill=0.0,
                               base=MAIN - 1, pattern=[[-1, P]], channel_multiplier=P).then_inc(s("side_rows_ready"), 1)
            pool.wait_ge(s("xvar_ready"), 1)
            pool.tensor_tensor(xrstd[:, 0:1], xvar[:, 0:1], minus_half[:, 0:1], ALU.pow).then_inc(s("xrstd_ready"), 1)
            pool.wait_ge(s("xvar_ready"), 2)
            pool.tensor_tensor(xrstd[:, 1:B], xvar[:, 1:B], minus_half[:, 1:B], ALU.pow).then_inc(s("xrstd_ready"), 1)

            pool.wait_ge(s("bo_ready"), 1)
            pool.tensor_tensor(x1[:, :, :], x1[:, :, :], bo_t[:, :].unsqueeze(1).broadcast_to([P, B, D]), ALU.add).then_inc(s("x1_ready"), 1)

            pool.iota(iota_p[:, :], pattern=[[0, 1]], base=0, channel_multiplier=1, allow_small_or_imprecise_dtypes=True)
            pool.iota(iota8[:, :, :], pattern=[[1, K], [0, 2 * HK]], base=0, channel_multiplier=0, allow_small_or_imprecise_dtypes=True)
            pool.iota(iota_hi[:, :, :], pattern=[[1, 2 * EC], [0, PAIRS]], base=0, channel_multiplier=0,
                      allow_small_or_imprecise_dtypes=True).then_inc(s("iota_ready"), 1)

            def iota_quarter(quarter):
                rows = slice(quarter * P // 4, (quarter + 1) * P // 4)
                pool.iota(iota_lo[:, rows, :], pattern=[[1, P // 4], [0, PAIRS]], base=quarter * P // 4, channel_multiplier=0,
                          allow_small_or_imprecise_dtypes=True).then_inc(s("iota_ready"), 1)

            def diagonals(t):
                pool.wait_ge(s("k_t_ready"), 2 * (t + 1))
                for g in range(G):
                    reuse(pool, "scores_ready", G * t + (g + 1 - G))
                    pool.tensor_tensor(k_diag[:, g, :, :], k_t[:, g, :].unsqueeze(1).broadcast_to([P, HG, P]),
                                       head_mask[:, :].unsqueeze(2).broadcast_to([P, HG, P]), ALU.mult).then_inc(s("k_diag_ready"), 1)

            def rstd_x1(t):
                pool.wait_ge(s("var1_ready"), t + 1)
                reuse(pool, "xn1_ready", t)
                link(pool.tensor_tensor(rstd1[:, :], var1[:, :], minus_half[:, 0:1], ALU.pow))
                wait_apart(pool, "pool_passed")
                pool.tensor_scalar(shift1[:, :], mv1[:, 0:1], rstd1[:, 0:1], -1.0, ALU.mult, ALU.mult).then_inc(s("rstd1_ready"), 1)

            def attention(t):
                if there(t + 1):
                    diagonals(t + 1)
                if there(t - 1):
                    rstd_x1(t - 1)
                for quarter, step in enumerate((0, 1, B - 2, B - 1)):
                    if at(t, step):
                        iota_quarter(quarter)

            steps(pool, attention, 2, chain, behind=1)

        @block.scalar
        def _(act):
            act.wait_ge(s("gate_in"), 32)
            act.activation(gate[:, :], gate_in[:, :], ACT.Tanh).then_inc(s("gate_ready"), 1)
            act.wait_ge(s("wb_in"), 16)

            def take_v(t):
                act.wait_ge(s("v_ps"), t + 1)
                if at(t, 0):
                    act.wait_ge(s("side_mask_ready"), 1)
                for side in range(2):
                    act.activation(v_ext[:, bass.ds(t, 1), :, side, 0:HD].rearrange("p b h d -> p (b h) d"),
                                   bank[2][:, 0:D].rearrange("p (h d) -> p h d", d=HD), ACT.Copy,
                                   scale=side_mask[:, side:side + 1]).then_inc(s("v_ready"), 1)

            def squares(t):
                act.wait_ge(s("qk_ready"), t + 1)
                reuse(act, "qk_ss_ready", t)
                act.activation(qk_sq[:, :, :], qk[:, :, :], ACT.Square).then_inc(s("qk_sq_ready"), 1)

            def take_qk(t):
                tq = bank[3][:, 0:D].rearrange("p (g c) -> p g c", c=P)
                tk = bank[3][:, D:2 * D].rearrange("p (g c) -> p g c", c=P)
                act.wait_ge(s("qk_t_ps"), t + 1)
                reuse(act, "k_diag_ready", G * t)
                act.activation(k_t[:, :, 0:MAIN], tk[:, :, 0:MAIN], ACT.Identity, scale=wb[:, 2:3], bias=wb[:, 3:4]).then_inc(s("k_t_ready"), 1)
                act.activation(k_t[:, :, MAIN:P], tk[:, :, MAIN:P], ACT.Identity, scale=wb[:, 4:5], bias=wb[:, 5:6]).then_inc(s("k_t_ready"), 1)
                reuse(act, "scores_ready", G * t)
                act.activation(q_t[:, :, :], tq, ACT.Identity, scale=wb[:, 0:1], bias=wb[:, 1:2]).then_inc(s("q_t_ready"), 1)

            def exps(t, g):
                hs = slice(g * HG, (g + 1) * HG)
                act.wait_ge(s("shifted_ready"), G * t + g + 1)
                reuse(act, "prob_t_ps", G * t + (g + 1 - G))
                act.activation(prob[:, hs, :], shifted[:, hs, :], ACT.Exp, scale=SCALE).then_inc(s("prob_ready"), 1)

            def take_prob(t, g):
                hs = slice(g * HG, (g + 1) * HG)
                act.wait_ge(s("prob_t_ps"), G * t + g + 1)
                reuse(act, "pv_ps", G * t + (g + 1 - G))
                act.activation(prob_t[:, hs, :].rearrange("p h c -> p (h c)"), wide[:, g * HG * P:(g + 1) * HG * P],
                               ACT.Copy).then_inc(s("prob_t_ready"), 1)

            def take_ctx(t):
                act.wait_ge(s("ctx_t_ps"), t + 1)
                reuse(act, "attn_ps", t)
                act.activation(ctx_t[:, :, :].rearrange("p g c -> p (g c)"), bank[3][:, 0:D], ACT.Copy).then_inc(s("ctx_t_ready"), 1)

            def norm_x1(t):
                act.wait_ge(s("rstd1_ready"), t + 1)
                reuse(act, "xn1_t_ps", t)
                act.activation(xn1[:, :].unsqueeze(1), x1[:, bass.ds(t, 1), :], ACT.Identity, scale=rstd1[:, 0:1],
                               bias=shift1[:, 0:1]).then_inc(s("xn1_ready"), 1)

            def take_xn1(t):
                act.wait_ge(s("xn1_t_ps"), t + 1)
                act.activation(xn1_t[:, :, bass.ds(t * P, P)], bank[xn1_bank(t)][:, 0:D].rearrange("p (g c) -> p g c", c=P),
                               ACT.Copy).then_inc(s("xn1_t_ready"), 1)

            def attention(t):
                if there(t - 1):
                    take_ctx(t - 1)
                if there(t):
                    exps(t, 1)
                if there(t + 1):
                    take_qk(t + 1)
                if there(t + 2):
                    squares(t + 2)
                if at(t, B - 1):
                    silu_up(0, 0)
                    silu_up(0, 1)
                if there(t):
                    take_prob(t, 0)
                    take_prob(t, 1)
                if at(t, B - 1):
                    take_hp(0)
                if there(t + 2):
                    take_v(t + 2)
                if there(t - 1) and not at(t, B):
                    norm_x1(t - 1)
                if there(t + 1):
                    exps(t + 1, 0)
                if there(t - 1) and not at(t, B):
                    take_xn1(t - 1)

            def take_simw():
                act.wait_ge(s("simw_ps"), 2)
                for side in range(2):
                    for odd in range(2):
                        act.activation(simw[:, side * NH * NK:(side + 1) * NH * NK].rearrange("p (h o k) -> p h o k", o=2, k=NK)[:, :, odd, :],
                                       bank[4 + side + 2 * odd][:, 0:NH // 2 * NK].rearrange("p (h k) -> p h k", k=NK), ACT.Copy).then_inc(s("simw_ready"), 1)

            def silu_up(t, half):
                if half == 0 and at(t, 0):
                    act.wait_ge(s("ffn_in"), 64)
                reuse(act, "down_ps", t)
                act.wait_ge(s("up_ps"), 2 * t + half + 1)
                for c in range(NC // 2):
                    i = half * NC // 2 + c
                    last = act.activation(h_t[:, i, :], bank[up_bank(t)[half]][:, c * P:(c + 1) * P], ACT.Silu, bias=bup_sb[:, i:i + 1])
                last.then_inc(s("h_t_ready"), 1)

            def take_hp(t):
                act.wait_ge(s("down_ps"), t + 1)
                act.activation(hp_t[:, bass.ds(t * P, P)], bank[down_bank(t)][:, 0:P], ACT.Identity, bias=bdown_sb[:, 0:1]).then_inc(s("hp_ready"), 1)
                reuse(act, "sim_ps", t)
                act.activation(hp[:, :], bank[down_bank(t)][:, 0:P], ACT.Identity, bias=bdown_sb[:, 0:1]).then_inc(s("hp_ready"), 1)

            def part_z(t, part, q):
                left = ("z_ps", "z_rest_ps", "z_low_ps")[part]
                if part == q == 0:
                    reuse(act, "z_sel_ps", 4 * t)
                act.wait_ge(s(left), 4 * t + q + 1)
                act.activation(z_part[:, part, :, 4 * q:4 * q + 4].rearrange("p t c -> p c t"),
                               bank[z_bank[q]].rearrange("p (c t) -> p c t", t=P),
                               ACT.Copy).then_inc(s(("z_top_ready", "z_mid_ready", "z_low_ready")[part]), 1)

            def exp_best(t):
                act.wait_ge(s("bshift_ready"), t + 1)
                reuse(act, "by_token_ready", t)
                act.activation(bexp[:, :, :], bshift[:, :, :], ACT.Exp).then_inc(s("bexp_ready"), 1)

            def take_by_k(t):
                act.wait_ge(s("by_k_ps"), t + 1)
                reuse(act, "pick_k_ready", t)
                reuse(act, "act_in_ready", t)
                for side in range(2):
                    rows = slice(side * PAIRS, (side + 1) * PAIRS)
                    src = bank[2].rearrange("p (i t) -> p i t", t=P)[rows, :, side * PAIRS:(side + 1) * PAIRS]
                    act.activation(lo_hi_k[rows, :, :], src[:, 0:2, :], ACT.Copy).then_inc(s("by_k_ready"), 1)
                    act.activation(prob_k[rows, :], src[:, 2, :], ACT.Copy).then_inc(s("by_k_ready"), 1)

            def tanh_act(t):
                act.wait_ge(s("act_in_ready"), t + 1)
                reuse(act, "wt_hi_ready", t)
                act.activation(act_tanh[:, :], act_in[:, :], ACT.Tanh, scale=0.5).then_inc(s("act_tanh_ready"), 1)

            def take_wt(t, q):
                if q == 0:
                    reuse(act, "out_ps", t)
                act.wait_ge(s("wt_e_ps"), 4 * t + q + 1)
                for side in range(2):
                    act.activation(
                        wt_e[:, :, side * PAIRS + q * QP:side * PAIRS + (q + 1) * QP].rearrange("p c j -> p j c"),
                        bank[scatter_bank(t)[q]].rearrange("p (j s c) -> p j s c", s=2, c=EC)[:, :, side, :],
                        ACT.Copy).then_inc(s("wt_e_ready"), 1)

            def numbers(t):
                act.wait_ge(s("part_ready"), t + 1)
                reuse(act, "by_k_ps", t)
                act.activation(by_token[:, 0, :, :], part_u[:, 0:1, :].broadcast_to([P, 2, HK]), ACT.Copy)
                act.activation(by_token[:, 1, 0, :], part_u[:, 1, :], ACT.Copy)
                act.activation(by_token[:, 1, 1, :], part_u[:, 1, :], ACT.Copy, bias=float(EC)).then_inc(s("numbers_ready"), 1)

            def experts(t):
                if there(t + 2):
                    silu_up(t + 2, 0)
                if there(t):
                    tanh_act(t)
                if there(t + 2):
                    silu_up(t + 2, 1)
                if there(t + 1):
                    part_z(t + 1, 0, 0)
                    part_z(t + 1, 0, 1)
                if at(t, -1):
                    norm_x1(B - 1)
                    take_xn1(B - 1)
                if there(t + 2):
                    take_hp(t + 2)
                if at(t, -1):
                    exp_best(0)
                    numbers(0)
                if there(t + 1):
                    for part, q in ((1, 0), (1, 1), (0, 2), (2, 0), (2, 1), (0, 3)):
                        part_z(t + 1, part, q)
                    take_by_k(t + 1)
                if at(t, B - 2):
                    for part, q in ((1, 2), (1, 3), (2, 2), (2, 3)):
                        part_z(B - 1, part, q)
                if there(t):
                    take_wt(t, 0)
                    take_wt(t, 1)
                if there(t + 1) and not at(t, B - 2):
                    part_z(t + 1, 1, 2)
                    part_z(t + 1, 1, 3)
                if there(t):
                    take_wt(t, 2)
                    take_wt(t, 3)
                if there(t + 1) and not at(t, B - 2):
                    part_z(t + 1, 2, 2)
                    part_z(t + 1, 2, 3)
                if there(t + 2):
                    exp_best(t + 2)
                    numbers(t + 2)

            steps(act, attention, 2, behind=1, before={-1: take_simw})
            steps(act, experts, 2, first=-1)

        @block.vector
        def _(dve):
            chain = Chain(dve, "dve_step")
            link = chain.link

            dve.wait_ge(s("wqkv_in"), 80)
            tensors = [wq_sb[:, 0, :], wq_sb[:, 1, :], wkv_sb[:, 0, 0:D], wkv_sb[:, 1, 0:D], bqk[:, 0:D], bqk[:, D:2 * D]]
            tensors = [a.rearrange("p (h d) -> p h d", d=HD) for a in tensors]
            for i, a in enumerate(tensors):
                last = dve.tensor_reduce(means[:, i, :], a, X, ALU.add)
            link(last)
            link(dve.tensor_scalar(means[:, :, :], means[:, :, :], 1.0 / HD, None, ALU.mult))
            for i, a in enumerate(tensors):
                last = dve.tensor_tensor(a, a, means[:, i, :].unsqueeze(2).broadcast_to([P, H, HD]), ALU.subtract)
            last.then_inc(s("wqk_ready"), 1)
            dve.wait_ge(s("x_in"), 16)

            def stats_x(tiles):
                for t in tiles:
                    last = dve.bn_stats(xstat[:, t, :], x1[:, t, :])
                link(last)
                for t in tiles:
                    last = dve.bn_aggr(xmv[:, t, :], xstat[:, t, :])
                link(last)
                cols = slice(tiles[0], tiles[-1] + 1)
                dve.tensor_scalar(xvar[:, cols], xmv[:, cols, 1], EPS_X, None, ALU.add).then_inc(s("xvar_ready"), 1)

            stats_x(range(1))
            dve.wait_ge(s("mean_ps"), 1)
            for g in range(G):
                last = dve.tensor_tensor(wq_sb[:, g, :], wq_sb[:, g, :], bank[0][:, 0:D], ALU.subtract)
            last.then_inc(s("wq_ready"), 1)
            stats_x(range(1, B))
            dve.wait_ge(s("side_mask_ready"), 1)
            link(dve.tensor_copy(v_ext[:, :, :, :, SUM].rearrange("p b h s -> p (b h) s"), side_mask[:, :].unsqueeze(1).broadcast_to([P, B * H, 2])))
            dve.wait_ge(s("gate_ready"), 1)
            dve.wait_ge(s("ident_ready"), 1)
            dve.tensor_scalar(minus_ident[:, :], ident[:, :], -1.0, None, ALU.mult).then_inc(s("minus_ident_ready"), 1)
            dve.tensor_scalar(half_gate[:, :], gate[:, 1:2], 0.5, None, ALU.mult)
            dve.tensor_scalar(bo_t[:, :], bo_t[:, :], gate[:, 0:1], None, ALU.mult).then_inc(s("bo_ready"), 1)

            def bias_qk(t):
                dve.wait_ge(s("qk_ps"), t + 1)
                if at(t, 0, 1):
                    dve.wait_ge(s("xrstd_ready"), t + 1)
                reuse(dve, "qkn_ready", t)
                dve.scalar_tensor_tensor(qk[:, 0:H, :].rearrange("p h d -> p (h d)"), bank[1][:, 0:D], xrstd[:, bass.ds(t, 1)], bqk[:, 0:D],
                                         ALU.mult, ALU.add)
                dve.tensor_tensor(qk[:, H:2 * H, :].rearrange("p h d -> p (h d)"), bank[1][:, D:2 * D], bqk[:, D:2 * D],
                                  ALU.add).then_inc(s("qk_ready"), 1)

            def var_qk(t, meanwhile):
                dve.wait_ge(s("qk_sq_ready"), t + 1)
                dve.tensor_reduce(qk_ss[:, :], qk_sq[:, :, :], X, ALU.add).then_inc(s("qk_ss_ready"), 1)
                dve.wait_ge(s("qk_ss_ready"), t + 1)
                link(dve.tensor_scalar(qk_var[:, :], qk_ss[:, :], 1.0 / HD, EPS_QK, ALU.mult, ALU.add), lambda: meanwhile(0))
                link(dve.tensor_scalar(qk_bits[:, :], qk_var[:, :].bitcast(i32), 1, None, ALU.arith_shift_right))
                link(dve.tensor_scalar(root[:, :].bitcast(i32), qk_bits[:, :], -1.0, float(0x5F3759DF), ALU.mult, ALU.add), lambda: meanwhile(1))
                for i in range(3):
                    link(dve.scalar_tensor_tensor(root_sq[:, :], root[:, :], -0.5, root[:, :], ALU.mult, ALU.mult))
                    if i == 0:
                        meanwhile(2)
                    link(dve.tensor_tensor(root_err[:, :], root_sq[:, :], qk_var[:, :], ALU.mult))
                    link(dve.scalar_tensor_tensor(root[:, :], root_err[:, :], 1.5, root[:, :], ALU.add, ALU.mult))

            def norm_qk(t):
                reuse(dve, "qk_t_ps", t)
                dve.tensor_tensor(qkn[:, :, :], qk[:, :, :], root[:, :].unsqueeze(2).broadcast_to([P, 2 * H, HD]),
                                  ALU.mult).then_inc(s("qkn_ready"), 1)

            def softmax_shift(t, g):
                hs = slice(g * HG, (g + 1) * HG)
                sc = wide[:, g * HG * P:(g + 1) * HG * P].rearrange("p (h k) -> p h k", k=KEYS)
                dve.wait_ge(s("scores_ready"), G * t + g + 1)
                for side, c0, c1 in sides:
                    last = dve.tensor_reduce(smax[:, side, hs], sc[:, :, c0:c1], X, ALU.max)
                link(last)
                reuse(dve, "prob_ready", G * t + (g + 1 - G))
                for side, c0, c1 in sides:
                    last = dve.tensor_tensor(shifted[:, hs, c0:c1], sc[:, :, c0:c1],
                                             smax[:, side, hs].unsqueeze(2).broadcast_to([P, HG, c1 - c0]), ALU.subtract)
                last.then_inc(s("shifted_ready"), 1)

            def take_context(t):
                pv = [bank[1 + g][:, 0:HG * 2 * (HD + 1)].rearrange("p (h s d) -> p h s d", h=HG, s=2) for g in range(G)]
                for g in range(G):
                    dve.wait_ge(s("pv_ps"), G * t + g + 1)
                    last = dve.reciprocal(rsum[:, g * HG:(g + 1) * HG, :], pv[g][:, :, :, SUM])
                link(last)
                for g in range(G):
                    hs = slice(g * HG, (g + 1) * HG)
                    reuse(dve, "ctx_ready", t)
                    last = dve.tensor_tensor(ctx_part[:, hs, :, :], pv[g][:, :, :, 0:HD],
                                             rsum[:, hs, :].unsqueeze(3).broadcast_to([P, HG, 2, HD]), ALU.mult)
                last.then_inc(s("pv_read"), 1)
                dve.wait_ge(s("pv_read"), t + 1)
                reuse(dve, "ctx_t_ps", t)
                dve.tensor_tensor(ctx_sb[:, :].rearrange("p (h d) -> p h d", d=HD), ctx_part[:, :, 0, :], ctx_part[:, :, 1, :],
                                  ALU.add).then_inc(s("ctx_ready"), 1)

            def residual(t):
                row = x1[:, bass.ds(t, 1), :]
                if at(t, 0):
                    dve.wait_ge(s("x1_ready"), 1)
                dve.wait_ge(s("attn_ps"), t + 1)
                dve.scalar_tensor_tensor(row, bank[0][:, 0:D].unsqueeze(1), gate[:, 0:1], row, ALU.mult, ALU.add).then_inc(s("x1_done"), 1)
                dve.wait_ge(s("x1_done"), t + 1)

            def stats_x1(t, part):
                if part == 0:
                    wait_apart(dve, "dve_passed")
                    return dve.bn_stats(stat1[:, :], x1[:, bass.ds(t, 1), :].rearrange("p a n -> p (a n)"))
                elif part == 1:
                    wait_apart(dve, "dve_passed")
                    reuse(dve, "rstd1_ready", t)
                    wait_apart(dve, "dve_passed")
                    return dve.bn_aggr(mv1[:, :], stat1[:, :])
                else:
                    return dve.tensor_scalar(var1[:, :], mv1[:, 1:2], EPS_X, None, ALU.add).then_inc(s("var1_ready"), 1)

            def attention(t):
                if there(t + 2):
                    bias_qk(t + 2)
                if there(t - 1):
                    residual(t - 1)
                if there(t + 2):
                    var_qk(t + 2, lambda part: stats_x1(t - 1, part) if there(t - 1) else None)
                    norm_qk(t + 2)
                elif there(t - 1):
                    for part in range(3):
                        if part:
                            link(last_stats)
                        last_stats = stats_x1(t - 1, part)
                if there(t + 1):
                    softmax_shift(t + 1, 0)
                if there(t):
                    take_context(t)
                if there(t + 1):
                    softmax_shift(t + 1, 1)

            def top_keys(t):
                dve.wait_ge(s("sim_ps"), t + 1)
                wait_apart(dve, "dve_passed")
                sims = [bank[sim_bank(t)[side]][:, h * NK:(h + 1) * NK] for side in range(2) for h in range(NH)]
                for i, sim in enumerate(sims):
                    last = dve.max(top_v[:, i, :], sim)
                link(last)
                wait_apart(dve, "dve_passed")
                for i, sim in enumerate(sims):
                    last = dve.max_index(top_i[:, i, :], top_v[:, i, :], sim)
                last.then_inc(s("top_ready"), 1)
                dve.tensor_tensor(sums[:, :, :, :], top_v[:, 0:NH, :].unsqueeze(3).broadcast_to([P, NH, K, K]),
                                  top_v[:, NH:2 * NH, :].unsqueeze(2).broadcast_to([P, NH, K, K]), ALU.add)
                dve.wait_ge(s("top_ready"), t + 1)
                link(dve.tensor_copy(top_f[:, :, :], top_i[:, :, :].rearrange("p g a -> p a g")))
                wait_apart(dve, "dve_passed")

            def top_experts(t):
                for h in range(NH):
                    last = dve.max(best[:, h, :], sums[:, h, :, :].rearrange("p a b -> p (a b)"))
                link(last)
                dve.tensor_tensor(bshift[:, :, :], best[:, :, :], best[:, :, 0:1].broadcast_to([P, NH, K]), ALU.subtract).then_inc(s("bshift_ready"), 1)
                for h in range(NH):
                    last = dve.max_index(pick[:, h, :], best[:, h, :], sums[:, h, :, :].rearrange("p a b -> p (a b)"))
                link(last)
                flat = pick[:, :, :].rearrange("p h k -> p (h k)")
                dve.tensor_scalar(pick2[:, 0, :], flat, 3, None, ALU.logical_shift_right)
                link(dve.tensor_scalar(pick2[:, 1, :], flat, K - 1, None, ALU.bitwise_and))
                link(dve.tensor_copy(pick2f[:, :].rearrange("p (k s h) -> p k s h", s=2, h=NH), pick2[:, :, :].rearrange("p s (h k) -> p k s h", k=K)))
                link(dve.tensor_tensor(one_hot[:, :, :], iota8[:, :, :], pick2f[:, :].unsqueeze(1).broadcast_to([P, K, 2 * HK]), ALU.is_equal))

                def sum_exps():
                    dve.wait_ge(s("bexp_ready"), t + 1)
                    dve.tensor_reduce(bsum[:, :], bexp[:, :, :], X, ALU.add)

                def invert_sums():
                    dve.reciprocal(brec[:, :], bsum[:, :])

                def probabilities():
                    reuse(dve, "by_k_ps", t)
                    for side in range(2):
                        last = dve.tensor_tensor(by_token[:, 2, side, :].rearrange("p (h k) -> p h k", k=K), bexp[:, :, :],
                                                 brec[:, :].unsqueeze(2).broadcast_to([P, NH, K]), ALU.mult)
                    last.then_inc(s("by_token_ready"), 1)

                link(dve.tensor_tensor(chosen[:, :, :].rearrange("p a (k g) -> p a k g", k=K), one_hot[:, :, :].rearrange("p a (k g) -> p a k g", k=K),
                                       top_f[:, :, :].unsqueeze(2).broadcast_to([P, K, K, 2 * NH]), ALU.mult))
                sum_exps()
                link(dve.tensor_reduce(side_i[:, :, :, :].rearrange("p k s h -> p (k s h)"), chosen[:, :, :].rearrange("p a x -> p x a"), X, ALU.add))
                invert_sums()
                link(dve.scalar_tensor_tensor(expert_u[:, :].rearrange("p (h k) -> p k h", k=K), side_i[:, :, 0, :], float(NK), side_i[:, :, 1, :],
                                              ALU.mult, ALU.add))
                reuse(dve, "numbers_ready", t)
                dve.tensor_scalar(part_u[:, 0, :], expert_u[:, :], P - 1, None, ALU.bitwise_and)
                dve.tensor_scalar(part_u[:, 1, :], expert_u[:, :], 7, None, ALU.logical_shift_right).then_inc(s("part_ready"), 1)
                probabilities()
                dve.wait_ge(s("part_ready"), t + 1)
                reuse(dve, "lo_stored", 32 * t)
                dve.tensor_copy(lo_bf[:, :], part_u[:, 0, :]).then_inc(s("lo_ready"), 1)

            def mask_rows(t):
                dve.wait_ge(s("lo_all_in"), 16 * (t + 1))
                reuse(dve, "z_sel_ps", 4 * t)
                dve.tensor_scalar(pick_r[:, :, :], lo_all[:, :, :], iota_p[:, 0:1], None, ALU.is_equal).then_inc(s("pick_r_ready"), 1)

            def mask_hi(t):
                dve.wait_ge(s("by_k_ready"), 4 * (t + 1))
                reuse(dve, "wt_hi_ready", t)
                dve.tensor_tensor(pick_hi[:, :, :], lo_hi_k[:, 1:2, :].broadcast_to([P, 2 * EC, PAIRS]), iota_hi[:, :, :],
                                  ALU.is_equal).then_inc(s("pick_hi_ready"), 1)

            def mask_k(t, quarter):
                rows = slice(quarter * P // 4, (quarter + 1) * P // 4)
                reuse(dve, "wt_e_ps", 4 * t)
                last = dve.tensor_tensor(pick_k[:, rows, :], lo_hi_k[:, 0:1, :].broadcast_to([P, P // 4, PAIRS]), iota_lo[:, rows, :], ALU.is_equal)
                if quarter == 3:
                    last.then_inc(s("pick_k_ready"), 1)

            def select_z(t):
                dve.wait_ge(s("pick_hi_ready"), t + 1)
                for q in range(4):
                    dve.wait_ge(s("z_sel_ps"), 4 * t + q + 1)
                    for side in range(2):
                        rows = slice(side * PAIRS, (side + 1) * PAIRS)
                        last = dve.tensor_tensor(z_sel[rows, q * QP:(q + 1) * QP, :],
                                                 bank[gather_bank(t)[q]].rearrange("p (j s c) -> p j s c", s=2, c=EC)[rows, :, side, :],
                                                 pick_hi[rows, side * EC:(side + 1) * EC, q * QP:(q + 1) * QP].rearrange("p c j -> p j c"), ALU.mult)
                    last.then_inc(s("z_sel_read"), 1)
                dve.wait_ge(s("z_sel_read"), 4 * (t + 1))
                link(dve.tensor_reduce(z_k[:, :], z_sel[:, :, :], X, ALU.add))
                dve.tensor_tensor(act_in[:, :], z_k[:, :], prob_k[:, :], ALU.mult).then_inc(s("act_in_ready"), 1)

            def weights(t, meanwhile):
                meanwhile(0)
                dve.wait_ge(s("act_tanh_ready"), t + 1)
                link(dve.scalar_tensor_tensor(wt[:, :], act_tanh[:, :], 1.0, act_in[:, :], ALU.add, ALU.mult), lambda: meanwhile(1))
                link(dve.tensor_copy(wt_part[:, 0, :], wt[:, :]))
                link(dve.tensor_tensor(wt_rest[:, :], wt[:, :], wt_part[:, 0, :], ALU.subtract), lambda: meanwhile(2))
                link(dve.tensor_copy(wt_part[:, 1, :], wt_rest[:, :]))
                reuse(dve, "wt_e_ps", 4 * t)
                link(dve.tensor_tensor(wt_part[:, 2, :], wt_rest[:, :], wt_part[:, 1, :], ALU.subtract), lambda: meanwhile(3))
                if at(t, B - 2):
                    mask_rows(B - 1)
                pieces = 4 if at(t, B - 1) else 1
                for i in range(pieces):
                    pairs = slice(i * PAIRS // pieces, (i + 1) * PAIRS // pieces)
                    for part in range(3):
                        last = dve.tensor_tensor(wt_hi[:, part, :, pairs], pick_hi[:, :, pairs],
                                                 wt_part[:, part:part + 1, pairs].broadcast_to([P, 2 * EC, PAIRS // pieces]), ALU.mult)
                    last.then_inc(s("wt_hi_ready"), 1)

            def finish(t):
                dve.wait_ge(s("out_ps"), t + 1)
                reuse(dve, "y_stored", 16 * t)
                dve.scalar_tensor_tensor(y_out[:, :].unsqueeze(1), bank[2][:, 0:D].unsqueeze(1), half_gate[:, 0:1], x1[:, bass.ds(t, 1), :],
                                         ALU.mult, ALU.add).then_inc(s("y_ready"), 1)

            def experts(t):
                if there(t):
                    select_z(t)
                    weights(t, lambda i: mask_k(t, i))
                if there(t + 1) and not at(t, -1):
                    if not at(t, B - 2):
                        mask_rows(t + 1)
                    mask_hi(t + 1)
                if there(t + 2):
                    top_keys(t + 2)
                    top_experts(t + 2)
                if at(t, -1):
                    mask_rows(0)
                    mask_hi(0)
                if at(t, B - 1):
                    finish(t - 1)
                if there(t) and not at(t, B - 2):
                    finish(t)

            def first_top_keys():
                dve.wait_ge(s("ctx_t_ps"), B)
                top_keys(0)

            steps(dve, attention, 2, chain, behind=1, before={B: first_top_keys})
            dve.wait_ge(s("iota_ready"), 5)
            top_experts(0)
            steps(dve, experts, 2, chain, first=-1)

        @block.tensor
        def _(pe):
            mm = pe.matmul

            def transpose(to, what):
                return pe.transpose(to, what, ident[:, :])

            def queries_keys(t):
                pe.wait_ge(s("tile_in"), 48 * (t + 1))
                reuse(pe, "qk_ready", t)
                reuse(pe, "pv_read", t - 2)
                for g in range(G):
                    mm(bank[1][:, 0:D], x_tile[:, g, :], wq_sb[:, g, :], start=g == 0, stop=g == G - 1)
                mm(bank[1][:, D:2 * D], y_main[:, :], wkv_sb[:, 0, 0:D], start=True, stop=False)
                mm(bank[1][:, D:2 * D], y_dca[:, :], wkv_sb[:, 1, 0:D], start=False, stop=True).then_inc(s("qk_ps"), 1)

            def values(t):
                if at(t, 0):
                    pe.wait_ge(s("bv_in"), 16)
                reuse(pe, "v_ready", 2 * t)
                mm(bank[2][:, 0:D], y_main[:, :], wkv_sb[:, 0, D:2 * D], start=True, stop=False)
                mm(bank[2][:, 0:D], y_dca[:, :], wkv_sb[:, 1, D:2 * D], start=False, stop=False)
                mm(bank[2][:, 0:D], side_rows[:, :], bv_sb[:, :], start=False, stop=True).then_inc(s("v_ps"), 1)

            def turn_qk(t):
                flat = qkn[:, :, :].rearrange("p h d -> p (h d)")
                pe.wait_ge(s("qkn_ready"), t + 1)
                reuse(pe, "ctx_t_ready", t - 1)
                reuse(pe, "q_t_ready", t)
                for i in range(2 * G):
                    last = transpose(bank[3][:, i * P:(i + 1) * P], flat[:, i * P:(i + 1) * P])
                last.then_inc(s("qk_t_ps"), 1)

            def scores(t, g):
                pe.wait_ge(s("q_t_ready"), t + 1)
                if at(t, 0):
                    pe.wait_ge(s("simw_ready"), 4)
                pe.wait_ge(s("k_diag_ready"), G * t + g + 1)
                reuse(pe, "prob_t_ready", G * t + (g + 1 - G))
                for half in range(2):
                    last = mm(bank[4 + 2 * g + half], q_t[:, g, :],
                              k_diag[:, g, half * HG // 2:(half + 1) * HG // 2, :].rearrange("p h c -> p (h c)"), start=True, stop=True)
                last.then_inc(s("scores_ready"), 1)

            def turn_prob(t, g):
                pe.wait_ge(s("prob_ready"), G * t + g + 1)
                for h in range(g * HG, (g + 1) * HG):
                    last = transpose(wide[:, h * P:(h + 1) * P], prob[:, h, :])
                last.then_inc(s("prob_t_ps"), 1)

            def context(t):
                pe.wait_ge(s("qk_ready"), min(t + 3, B) if isinstance(t, int) else t + 3)
                pe.wait_ge(s("v_ready"), 2 * min(t + 3, B) if isinstance(t, int) else 2 * (t + 3))
                for g in range(G):
                    pe.wait_ge(s("prob_t_ready"), G * t + g + 1)
                    for h in range(HG):
                        last = mm(bank[1 + g][:, h * 2 * (HD + 1):(h + 1) * 2 * (HD + 1)], prob_t[:, g * HG + h, :],
                                  v_ext[:, bass.ds(t, 1), g * HG + h, :, :].rearrange("p b s d -> p (b s d)"), start=True, stop=True)
                    last.then_inc(s("pv_ps"), 1)

            def turn_ctx(t):
                pe.wait_ge(s("ctx_ready"), t + 1)
                pe.wait_ge(s("q_t_ready"), min(t + 2, B) if isinstance(t, int) else t + 2)
                reuse(pe, "xn1_t_ready", t)
                for g in range(G):
                    last = transpose(bank[3][:, g * P:(g + 1) * P], ctx_sb[:, g * P:(g + 1) * P])
                last.then_inc(s("ctx_t_ps"), 1)

            def project(t):
                if at(t, 0):
                    pe.wait_ge(s("wo_in"), 16)
                pe.wait_ge(s("ctx_t_ready"), t + 1)
                reuse(pe, "x1_done", t)
                for g in range(G):
                    last = mm(bank[0][:, 0:D], ctx_t[:, g, :], wo_sb[:, g, :], start=g == 0, stop=g == G - 1)
                last.then_inc(s("attn_ps"), 1)

            def turn_xn1(t):
                pe.wait_ge(s("xn1_ready"), t + 1)
                pe.wait_ge(s("q_t_ready"), min(t + 3, B) if isinstance(t, int) else t + 3)
                pe.wait_ge(s("ctx_t_ready"), t + 1)
                if at(t, B - 1):
                    pe.wait_ge(s("x1_done"), B)
                for g in range(G):
                    last = transpose(bank[xn1_bank(t)][:, g * P:(g + 1) * P], xn1[:, g * P:(g + 1) * P])
                last.then_inc(s("xn1_t_ps"), 1)

            def attention(t):
                if there(t + 2):
                    queries_keys(t + 2)
                if there(t - 1):
                    project(t - 1)
                if there(t + 1):
                    turn_qk(t + 1)
                if at(t, B - 1):
                    layer_up(0)
                if there(t):
                    turn_prob(t, 0)
                    turn_prob(t, 1)
                if there(t + 2):
                    values(t + 2)
                if there(t + 1):
                    scores(t + 1, 0)
                if at(t, B - 1):
                    layer_down(0)
                if there(t):
                    context(t)
                if at(t, B - 1):
                    similarities(0)
                if there(t - 1) and not at(t, B):
                    turn_xn1(t - 1)
                if there(t + 1):
                    scores(t + 1, 1)
                if there(t):
                    turn_ctx(t)

            pe.wait_ge(s("ident_ready"), 1)
            pe.wait_ge(s("wqk_ready"), 1)
            pe.wait_ge(s("mean_w_ready"), 1)
            for g in range(G):
                last = mm(bank[0][:, 0:D], mean_w[:, :], wq_sb[:, g, :], start=g == 0, stop=g == G - 1)
            last.then_inc(s("mean_ps"), 1)

            def fold_keys():
                pe.wait_ge(s("ret_in"), 32)
                for i in range(2 * NH):
                    rows = slice(i % 2 * (P // 2), (i % 2 + 1) * (P // 2))
                    h = i % NH // 2
                    last = mm(bank[4 + i // NH + i % 2 * 2][:, h * NK:(h + 1) * NK], wret_sb[rows, i // 2, :], keys_sb[rows, i // 2, :], start=True, stop=True)
                    if i >= 2 * NH - 2:
                        last.then_inc(s("simw_ps"), 1)

            def layer_up(t):
                if at(t, 0):
                    pe.wait_ge(s("ffn_in"), 64)
                    pe.wait_ge(s("xn1_t_ready"), 1)
                    pe.wait_ge(s("pv_read"), B - 1)
                if at(t, 1):
                    pe.wait_ge(s("ctx_t_ready"), B)
                reuse(pe, "z_low_ready", 4 * (t - 1))
                for half in range(2):
                    if half == 1 and at(t, 1):
                        pe.wait_ge(s("top_ready"), 1)
                    for c in range(NC // 2):
                        i = half * NC // 2 + c
                        for d in range(G):
                            last = mm(bank[up_bank(t)[half]][:, c * P:(c + 1) * P], wup_sb[:, d, i * P:(i + 1) * P], xn1_t[:, d, bass.ds(t * P, P)],
                                      start=d == 0, stop=d == G - 1)
                    last.then_inc(s("up_ps"), 1)

            def layer_down(t):
                pe.wait_ge(s("h_t_ready"), 2 * (t + 1))
                if at(t, 0):
                    pe.wait_ge(s("x1_done"), B - 1)
                reuse(pe, "by_k_ready", 4 * (t - 1))
                reuse(pe, "y_ready", t - 2)
                for c in range(NC):
                    last = mm(bank[down_bank(t)][:, 0:P], wdown_sb[:, c, :], h_t[:, c, :], start=c == 0, stop=c == NC - 1)
                last.then_inc(s("down_ps"), 1)

            def similarities(t):
                pe.wait_ge(s("hp_ready"), 2 * (t + 1))
                if at(t, 1):
                    pe.wait_ge(s("xn1_t_ready"), B)
                reuse(pe, "top_ready", t)
                for side in range(2):
                    last = mm(bank[sim_bank(t)[side]][:, 0:NH * NK], hp[:, :], simw[:, side * NH * NK:(side + 1) * NH * NK], start=True, stop=True)
                last.then_inc(s("sim_ps"), 1)

            def inner(t, q):
                if q == 0:
                    reuse(pe, "z_sel_read", 4 * t)
                if q >= 2 and there(t + 1):
                    pe.wait_ge(s("h_t_ready"), 2 * t + (q + 1))
                elif q >= 2:
                    reuse(pe, "z_low_ready", 4 * t)
                for c in range(4):
                    last = mm(bank[z_bank[q]][:, c * P:(c + 1) * P], down_sb[:, 4 * q + c, :], hp_t[:, bass.ds(t * P, P)],
                              start=c == 0, stop=c == 3, skip_group_check=True)
                last.then_inc(s("z_ps"), 1)

            def take_off(t, part, q):
                pe.wait_ge(s(("z_top_ready", "z_mid_ready")[part]), 4 * t + q + 1)
                mm(bank[z_bank[q]].rearrange("p (c t) -> p c t", t=P), minus_ident[:, :], z_part[:, part, :, 4 * q:4 * q + 4].rearrange("p t c -> p c t"),
                   start=False, stop=True, skip_group_check=True).then_inc(s(("z_rest_ps", "z_low_ps")[part]), 1)

            def turn_by_token(t):
                pe.wait_ge(s("by_token_ready"), t + 1)
                pe.wait_ge(s("numbers_ready"), t + 1)
                if there(t + 1):
                    pe.wait_ge(s("hp_ready"), 2 * (t + 2))
                for i in range(3):
                    last = transpose(bank[2][:, i * P:(i + 1) * P], by_token[:, i, :, :].rearrange("p s k -> p (s k)"))
                last.then_inc(s("by_k_ps"), 1)

            def gather(t):
                pe.wait_ge(s("pick_r_ready"), t + 1)
                pe.wait_ge(s("z_low_ready"), 4 * (t + 1))
                reuse(pe, "wt_e_ready", 8 * (t - 1) if at(t, B - 1) else 8 * t)
                for q in range(4):
                    if q == 3 and not at(t, B - 1):
                        pe.wait_ge(s("z_sel_read"), 4 * t + 1)
                    for j in range(QP):
                        pair = q * QP + j
                        for part in range(3):
                            last = mm(bank[gather_bank(t)[q]][:, j * 2 * EC:(j + 1) * 2 * EC].rearrange("p (s c) -> p s c", c=EC), pick_r[:, pair, :],
                                      z_part[:, part, :, :].rearrange("p (s j) c -> p s j c", s=2)[:, :, pair, :], start=part == 0, stop=part == 2)
                    last.then_inc(s("z_sel_ps"), 1)

            def scatter(t, q):
                if q == 0:
                    pe.wait_ge(s("wt_hi_ready"), t + 1)
                    pe.wait_ge(s("z_sel_read"), 4 * (t + 1))
                    if there(t + 1):
                        pe.wait_ge(s("z_low_ready"), 4 * t + 6)
                    if at(t, B - 2):
                        pe.wait_ge(s("top_ready"), B)
                if at(t, B - 1):
                    pe.wait_ge(s("wt_hi_ready"), t + 1 + q)
                if q == 3:
                    pe.wait_ge(s("wt_e_ready"), 8 * t + 2)
                for j in range(QP):
                    pair = q * QP + j
                    for part in range(3):
                        last = mm(bank[scatter_bank(t)[q]][:, j * 2 * EC:(j + 1) * 2 * EC], pick_k[:, :, pair], wt_hi[:, part, :, pair],
                                  start=part == 0, stop=part == 2)
                last.then_inc(s("wt_e_ps"), 1)

            def combine(t):
                pe.wait_ge(s("wt_e_ready"), 8 * (t + 1))
                reuse(pe, "y_ready", t)
                pe.wait_ge(s("by_k_ready"), 4 * min(t + 2, B) if isinstance(t, int) else 4 * (t + 2))
                for c in range(EC):
                    last = mm(bank[2][:, 0:D], wt_e[:, c, :], up_sb[:, c, :], start=c == 0, stop=c == EC - 1)
                last.then_inc(s("out_ps"), 1)

            def experts(t):
                if there(t + 2):
                    layer_up(t + 2)
                if there(t + 1):
                    inner(t + 1, 0)
                    inner(t + 1, 1)
                if at(t, -1):
                    turn_xn1(B - 1)
                if there(t + 2):
                    layer_down(t + 2)
                if there(t + 1):
                    take_off(t + 1, 0, 0)
                    take_off(t + 1, 0, 1)
                    inner(t + 1, 2)
                if there(t + 2):
                    similarities(t + 2)
                if there(t + 1):
                    take_off(t + 1, 1, 0)
                    take_off(t + 1, 1, 1)
                    inner(t + 1, 3)
                    turn_by_token(t + 1)
                if at(t, B - 2):
                    for part, q in ((0, 2), (0, 3), (1, 2), (1, 3)):
                        take_off(B - 1, part, q)
                    gather(B - 1)
                if there(t):
                    scatter(t, 0)
                    scatter(t, 1)
                if there(t + 1) and not at(t, B - 2):
                    take_off(t + 1, 0, 2)
                    take_off(t + 1, 0, 3)
                if there(t):
                    scatter(t, 2)
                    scatter(t, 3)
                if there(t + 1) and not at(t, B - 2):
                    take_off(t + 1, 1, 2)
                    take_off(t + 1, 1, 3)
                if there(t):
                    combine(t)
                if there(t + 1) and not at(t, B - 2):
                    gather(t + 1)

            pe.wait_ge(s("wq_ready"), 1)
            pe.wait_ge(s("side_rows_ready"), 1)
            steps(pe, attention, 2, behind=1, before={-1: fold_keys})
            pe.wait_ge(s("experts_in"), 32)
            pe.wait_ge(s("minus_ident_ready"), 1)
            steps(pe, experts, 2, first=-1)


def kernel(**inputs):
    import numpy as np
    import concourse.bacc as bacc
    from concourse import mybir as _mybir
    from concourse.bass_utils import run_bass_kernel_spmd

    a = {k.removeprefix("L0_"): np.asarray(v) for k, v in inputs.items()}
    D, H, HD, P, DCA = 256, 16, 16, 128, 16

    def heads_apart(w):
        return w.reshape(*w.shape[:-1], H, 2, HD).swapaxes(-3, -2).reshape(*w.shape[:-1], 2 * D)

    xn = [a["xattn_qn_w"], a["xattn_qn_b"], a["xattn_kn_w"], a["xattn_kn_b"], a["xattn_kn_dca_w"], a["xattn_kn_dca_b"]]
    keys = a["ffn_keys"].transpose(2, 0, 3, 1)
    keys = keys.reshape(8, P, keys.shape[3]).transpose(1, 0, 2)
    laid = {
        "x": a["x"],
        "x_t": a["x"].reshape(8, P, D // P, P).transpose(0, 3, 2, 1),
        "y_t": a["ctx_1024"].swapaxes(1, 2),
        "gates": np.concatenate([a["g_xattn"], a["g_ffn"]]),
        "w_q": a["xattn_Wq"],
        "b_q": a["xattn_bq"],
        "w_kv": np.stack([heads_apart(np.concatenate([a["xattn_Wk"], a["xattn_Wv"]], 1)), a["xattn_Wkv_dca"]]),
        "b_kv": np.stack([heads_apart(np.concatenate([a["xattn_bk"], a["xattn_bv"]])), a["xattn_bkv_dca"]]),
        "ln_wb": np.stack([np.tile(v, P // HD) for v in xn], 1),
        "w_o": a["xattn_Wo"],
        "b_o": a["xattn_bo"],
        "w_up_t": a["ffn_W_up"].T,
        "b_up": a["ffn_b_up"].reshape(-1, P).T,
        "w_down_t": a["ffn_W_down"].T,
        "b_down": a["ffn_b_down"].reshape(P, 1),
        "w_ret": a["ffn_W_q"],
        "keys_t": keys,
        "down_t": a["ffn_down_embed"].T,
        "up": a["ffn_up_embed"],
    }
    nc = bacc.Bacc("TRN2", target_bir_lowering=False, num_devices=1)
    arrays, args = {}, []
    for name, v in laid.items():
        v = np.ascontiguousarray(v)
        arrays[name] = v
        args.append(nc.dram_tensor(name, v.shape, _mybir.dt.from_np(v.dtype), kind="ExternalInput").ap())
    scratch = nc.dram_tensor("lo_scratch", (8, 64, 2, 64), _mybir.dt.bfloat16, kind="Internal").ap()
    out = nc.dram_tensor("out", (8, P, D), _mybir.dt.float32, kind="ExternalOutput").ap()
    gated_xattn_peer_kernel(nc, *args, scratch, out)
    r = run_bass_kernel_spmd(nc, [arrays], core_ids=[0])
    return r.results[0]["out"]
```
